# Optimizing a Trainium2 kernel written in Bass

```python
import numpy as np
import jax
import jax.numpy as jnp

def _softmax(x, axis=-1):
    return jax.nn.softmax(x, axis=axis)

def _gelu(x):
    return jax.nn.gelu(x, approximate=True)

def _silu(x):
    return jax.nn.silu(x)

def _sigmoid(x):
    return jax.nn.sigmoid(x)

def _layernorm(x, axis=-1, eps=1e-05):
    m = jnp.mean(x, axis=axis, keepdims=True)
    v = jnp.var(x, axis=axis, keepdims=True)
    return (x - m) / jnp.sqrt(v + eps)

def _scatter_add(tgt, idx, src, axis=0):
    return tgt.at[idx].add(src)

def _segment_sum(src, seg, n):
    return jax.ops.segment_sum(src, seg, n)
kernel_name = 'mk_vit_tower_postln_d1_tok_img1024_r4_00a1e9'

def setup_inputs(seed: int=0):
    np.random.seed(seed)
    _w = jnp.asarray

    def _rec_inputs():
        import jax
        import jax.numpy as jnp
        _rk = jax.random.key(seed)
        x = jax.random.uniform(jax.random.fold_in(_rk, 1), (8, 3, 256, 256), jnp.float32, 0.0, 1)
        return x
    x = _rec_inputs()

    def _L0_tok_setup():
        import jax, jax.numpy as jnp
        import numpy as np
        _GRAY_W = (0.2989, 0.587, 0.114)
        key = jax.random.key(seed)
        x = jax.random.uniform(key, (32, 3, 256, 256), dtype=jnp.float32)
        sx = jnp.array([[-3.0, 0.0, 3.0], [-10.0, 0.0, 10.0], [-3.0, 0.0, 3.0]], dtype=jnp.float32)
        scharr = jnp.stack([sx, sx.T])[:, None, :, :]
        return {'x': x, 'scharr': scharr}
    _L0_tok_all = _L0_tok_setup()
    _L0_tok_in = {k: v for k, v in _L0_tok_all.items() if k in ('scharr',)}
    del _L0_tok_all

    def _L0_attn_setup():
        import jax, jax.numpy as jnp
        import numpy as np
        B, L, D_MODEL, D_STATE = (8, 1024, 256, 64)
        key = jax.random.key(seed)
        k1, k2, k3, k4 = jax.random.split(key, 4)
        u = jax.random.normal(k1, (B, L, D_MODEL), dtype=jnp.float32)
        A_log = jnp.log(jnp.arange(1, D_STATE + 1, dtype=jnp.float32))
        D = jax.random.normal(k2, (D_MODEL,), dtype=jnp.float32)
        C_re = jax.random.normal(k3, (D_MODEL, D_STATE), dtype=jnp.float32)
        C_im = jax.random.normal(k4, (D_MODEL, D_STATE), dtype=jnp.float32)
        log_dt = jnp.log(jnp.full((D_MODEL,), 0.01, dtype=jnp.float32))
        return {'u': u, 'A_log': A_log, 'D': D, 'C_re': C_re, 'C_im': C_im, 'log_dt': log_dt}
    _L0_attn_all = _L0_attn_setup()
    _L0_attn_in = {k: v for k, v in _L0_attn_all.items() if k in ('A_log', 'D', 'C_re', 'C_im', 'log_dt')}
    del _L0_attn_all

    def _L0_ffn_setup():
        import jax, jax.numpy as jnp
        import numpy as np
        B, T, C = (2, 128, 256)
        I = 1024
        E = 8
        K = 2
        key = jax.random.key(seed)
        ks = jax.random.split(key, 8)
        s = 0.02
        return {'x': jax.random.normal(ks[0], (B, T, C), jnp.float32), 'Wr1': jax.random.normal(ks[1], (C, C // 4), jnp.float32) * s, 'br1': jnp.zeros((C // 4,), jnp.float32), 'Wr2': jax.random.normal(ks[2], (C // 4, E), jnp.float32) * s, 'br2': jnp.zeros((E,), jnp.float32), 'Ws1': jax.random.normal(ks[3], (C, I), jnp.float32) * s, 'bs1': jnp.zeros((I,), jnp.float32), 'Ws2': jax.random.normal(ks[4], (I, C), jnp.float32) * s, 'bs2': jnp.zeros((C,), jnp.float32), 'We1': jax.random.normal(ks[5], (E, C, I), jnp.float32) * s, 'be1': jnp.zeros((E, I), jnp.float32), 'We2': jax.random.normal(ks[6], (E, I, C), jnp.float32) * s, 'be2': jnp.zeros((E, C), jnp.float32)}
    _L0_ffn_all = _L0_ffn_setup()
    _L0_ffn_in = {k: v for k, v in _L0_ffn_all.items() if k in ('Wr1', 'br1', 'Wr2', 'br2', 'Ws1', 'bs1', 'Ws2', 'bs2', 'We1', 'be1', 'We2', 'be2')}
    del _L0_ffn_all
    return {'x': x, 'L0_tok_scharr': _L0_tok_in['scharr'], 'L0_attn_A_log': _L0_attn_in['A_log'], 'L0_attn_D': _L0_attn_in['D'], 'L0_attn_C_re': _L0_attn_in['C_re'], 'L0_attn_C_im': _L0_attn_in['C_im'], 'L0_attn_log_dt': _L0_attn_in['log_dt'], 'L0_ffn_Wr1': _L0_ffn_in['Wr1'], 'L0_ffn_br1': _L0_ffn_in['br1'], 'L0_ffn_Wr2': _L0_ffn_in['Wr2'], 'L0_ffn_br2': _L0_ffn_in['br2'], 'L0_ffn_Ws1': _L0_ffn_in['Ws1'], 'L0_ffn_bs1': _L0_ffn_in['bs1'], 'L0_ffn_Ws2': _L0_ffn_in['Ws2'], 'L0_ffn_bs2': _L0_ffn_in['bs2'], 'L0_ffn_We1': _L0_ffn_in['We1'], 'L0_ffn_be1': _L0_ffn_in['be1'], 'L0_ffn_We2': _L0_ffn_in['We2'], 'L0_ffn_be2': _L0_ffn_in['be2']}

def reference(x, L0_tok_scharr, L0_attn_A_log, L0_attn_D, L0_attn_C_re, L0_attn_C_im, L0_attn_log_dt, L0_ffn_Wr1, L0_ffn_br1, L0_ffn_Wr2, L0_ffn_br2, L0_ffn_Ws1, L0_ffn_bs1, L0_ffn_Ws2, L0_ffn_bs2, L0_ffn_We1, L0_ffn_be1, L0_ffn_We2, L0_ffn_be2):
    import jax
    import jax.numpy as jnp

    def _L0_tok_ref(x, scharr):
        import jax, jax.numpy as jnp
        import numpy as np
        _GRAY_W = (0.2989, 0.587, 0.114)
        w = jnp.asarray(_GRAY_W, dtype=x.dtype)
        gray = jnp.einsum('bchw,c->bhw', x, w)[:, None]
        edges = jax.lax.conv_general_dilated(gray, scharr, window_strides=(1, 1), padding='SAME', dimension_numbers=('NCHW', 'OIHW', 'NCHW'))
        abs_edges = jnp.sqrt(jnp.square(edges))
        edge = abs_edges.sum(axis=1) / 2
        return edge

    def _L0_attn_ref(u, A_log, D, C_re, C_im, log_dt):
        import jax, jax.numpy as jnp
        import numpy as np
        B, L, D_MODEL, D_STATE = (8, 1024, 256, 64)
        L_ = u.shape[1]
        dt = jnp.exp(log_dt)
        A = -jnp.exp(A_log)
        t = jnp.arange(L_, dtype=u.dtype)
        at = dt[:, None, None] * A[None, None, :] * t[None, :, None]
        K = jnp.einsum('mn,mln->ml', C_re, jnp.exp(at))
        u_f = jnp.fft.rfft(u.transpose(0, 2, 1), n=2 * L_)
        k_f = jnp.fft.rfft(K, n=2 * L_)
        y = jnp.fft.irfft(u_f * k_f, n=2 * L_)[..., :L_]
        return y.transpose(0, 2, 1) + u * D

    def _L0_ffn_ref(x, Wr1, br1, Wr2, br2, Ws1, bs1, Ws2, bs2, We1, be1, We2, be2):
        import jax, jax.numpy as jnp
        import numpy as np
        B, T, C = (2, 128, 256)
        I = 1024
        E = 8
        K = 2
        Bb, Tt, Cc = x.shape
        xf = x.reshape(-1, Cc)
        logits = jax.nn.relu(xf @ Wr1 + br1) @ Wr2 + br2
        gates = jax.nn.softmax(logits, axis=-1)
        tg, ti = jax.lax.top_k(gates, K)
        tg = jax.nn.softmax(tg / K, axis=-1)
        out = jax.nn.silu(xf @ Ws1 + bs1) @ Ws2 + bs2
        for e in range(E):
            h = jax.nn.silu(xf @ We1[e] + be1[e]) @ We2[e] + be2[e]
            w = jnp.sum(tg * (ti == e), axis=-1)
            out = out + w[:, None] * h
        return out.reshape(Bb, Tt, Cc)
    h = _L0_tok_ref(x, L0_tok_scharr)
    h = _layernorm(h + _L0_attn_ref(h, L0_attn_A_log, L0_attn_D, L0_attn_C_re, L0_attn_C_im, L0_attn_log_dt), axis=-1)
    h = _layernorm(h + _L0_ffn_ref(h, L0_ffn_Wr1, L0_ffn_br1, L0_ffn_Wr2, L0_ffn_br2, L0_ffn_Ws1, L0_ffn_bs1, L0_ffn_Ws2, L0_ffn_bs2, L0_ffn_We1, L0_ffn_be1, L0_ffn_We2, L0_ffn_be2), axis=-1)
    return h

_drawn_inputs = setup_inputs


def setup_inputs(seed=0):
    import zlib

    import numpy as np

    out = dict(_drawn_inputs(seed))
    spreads = {'L0_attn_log_dt': (-4.605170249938965, 0.2),
     'L0_ffn_br1': (0.0, 0.8),
     'L0_ffn_br2': (0.0, 0.425),
     'L0_ffn_bs1': (0.0, 0.1),
     'L0_ffn_bs2': (0.0, 0.1),
     'L0_ffn_be1': (0.0, 0.354),
     'L0_ffn_be2': (0.0, 0.1)}
    factors = {'L0_attn_D': 4.018, 'L0_ffn_Wr2': 8.0}
    for name, (base, spread) in spreads.items():
        noise = np.random.default_rng([zlib.crc32(name.encode()), seed]).standard_normal(out[name].shape)
        drawn = base * np.exp(spread * noise) if base else spread * noise
        out[name] = jnp.asarray(drawn.astype(out[name].dtype))
    for name, factor in factors.items():
        out[name] = (out[name] * factor).astype(out[name].dtype)
    return out
```

```python
from contextlib import ExitStack

import concourse.bass as bass
import numpy as np
from concourse import mybir

F32 = mybir.dt.float32
F32R = mybir.dt.float32r
I32 = mybir.dt.int32
U32 = mybir.dt.uint32
ALU = mybir.AluOpType
ACT = mybir.ActivationFunctionType
X = mybir.AxisListType.X

P = 128
B, COLORS, L, M = 8, 3, 256, 256
LH = L // P
TILES = B * LH
PAIRS = B // 2
W2 = 2 * M
N_STATE = 64
MP = M // 2
E_CH = 16
N_CH = MP // E_CH
NDFT = 2 * L
KC = L // P
GRAY = (0.2989, 0.587, 0.114)
EPS = 1e-5

TOKENS = B * L
E, K_TOP = 8, 2
I, IC = 1024, 8
PAIRS1 = IC // 2
R1 = M // 4
T = 256
SHARED = TOKENS // T
SLOTS = K_TOP * TOKENS // T + E - 1
SLOTS += SLOTS % 2
GR = 8
SMALL = 9 * P + E * E
SOFT, SOFT2 = 4, 21


def shape_constants():
    ang = np.pi * ((2 * np.arange(L)[None, :] + 1) * np.arange(L)[:, None] % (2 * NDFT)) / NDFT
    fwd = np.stack([np.cos(ang), -np.sin(ang)], 1)
    fwd = fwd.reshape(LH, P, 2, KC, P).transpose(1, 0, 3, 2, 4)
    inv = np.stack([np.cos(ang.T), -np.sin(ang.T)], 1) * (2.0 / NDFT)
    inv = inv.reshape(KC, P, 2, L).transpose(1, 0, 2, 3)
    row, col = np.arange(P)[:, None], np.arange(P)[None, :]
    bands = [(row - col == dy - 1) for dy in range(3)]
    ident = row == col
    before = row < col
    ones = np.ones((P, P))
    ramp = np.broadcast_to(col, (P, P))
    seam = np.zeros((P, 2, P))
    seam[0:3, 0, P - 1] = 1
    seam[3:6, 1, 0] = 1
    upto = np.broadcast_to((np.arange(E)[None, :] <= np.arange(E)[:, None]).reshape(1, -1), (P, E * E))
    small = np.concatenate([np.stack(bands + [ident, before, ones, ramp], 1).reshape(P, -1),
                            seam.reshape(P, -1), upto], 1)
    return (np.ascontiguousarray(fwd.reshape(P, -1), np.float32),
            np.ascontiguousarray(inv.reshape(P, -1), np.float32), np.ascontiguousarray(small, np.float32))


def front(nc, A, keep):
    hln, xT = keep["hln"], keep["xT"]
    small, eps_t = keep["small"], keep["eps"]
    BAND = [small[:, i * P:(i + 1) * P] for i in range(3)]
    IDENT = small[:, 3 * P:4 * P]
    RAMP = small[:, 6 * P:7 * P]
    SEAM = [small[0:6, (7 + i) * P:(8 + i) * P] for i in range(2)]
    with ExitStack() as ctx:
        def sb(name, shape, dt=F32):
            return ctx.enter_context(nc.sbuf_tensor(name, shape, dt))

        def sem(name):
            return ctx.enter_context(nc.semaphore(name))

        NX = 3
        image = sb("image", [P, NX, COLORS, LH, M])
        gray = sb("gray", [P, LH, B, M + 2])
        edge_rows = sb("edge_rows", [6, B, M])
        fwd = sb("fwd", [P, LH, 2 * KC, P])
        inv = sb("inv", [P, KC, 2, L])
        taps = sb("taps", [P, 2, 3, 3])
        seam_taps = sb("seam_taps", [6, 2])
        stencil = sb("stencil", [P, 2, 3, P])
        seam = sb("seam", [6, 2, 2, P])
        half_abs = sb("half_abs", [P, 2, 2, W2])
        h = sb("h", [P, LH, PAIRS, W2])
        log_dt = sb("log_dt", [P, MP])
        a_log = sb("a_log", [P, 1])
        a_exp = sb("a_exp", [P, 1])
        dt_exp = sb("dt_exp", [P, MP])
        neg_dta = sb("neg_dta", [P, MP])
        far = sb("far", [P, MP])
        c_in = sb("c_in", [P, 2, N_STATE])
        c_decay = sb("c_decay", [P, MP, 2, 2])
        decay = sb("decay", [P, 2, E_CH, P])
        d_row = sb("d_row", [1, M])
        zero = sb("zero", [P, SLOTS * T * M // P // 12])
        taps_k = sb("taps_k", [P, LH, 2, MP])
        kf = sb("kf", [P, 2 * KC, M])
        prod = sb("prod", [P, 2, 4, W2])
        spec = sb("spec", [P, 2, KC, 2, W2])
        stats = sb("stats", [P, TILES, 6])
        mv = sb("mv", [P, TILES, 2])
        sd = sb("sd", [P, TILES])
        rstd = sb("rstd", [P, TILES])

        bank = keep["bank"]

        s_const = sem("s_const")
        s_dft = sem("s_dft")
        s_par = sem("s_par")
        s_image = [sem(f"s_image{i}") for i in range(NX)]
        s_pad = sem("s_pad")
        s_gray1 = sem("s_gray1")
        s_gray2 = sem("s_gray2")
        s_gray = sem("s_gray")
        s_rows = [sem(f"s_rows{i}") for i in range(PAIRS)]
        s_st0 = sem("s_st0")
        s_stencil = sem("s_stencil")
        s_edge = sem("s_edge")
        s_abs = sem("s_abs")
        s_h = sem("s_h")
        s_exp0 = sem("s_exp0")
        s_dta = sem("s_dta")
        s_far = sem("s_far")
        s_ct = sem("s_ct")
        s_cz = sem("s_cz")
        s_cd = sem("s_cd")
        s_arg = [sem("s_arg_even"), sem("s_arg_odd")]
        s_decay = sem("s_decay")
        s_ksum = sem("s_ksum")
        s_kcopy = sem("s_kcopy")
        s_kd = sem("s_kd")
        s_kf = sem("s_kf")
        s_kfc = sem("s_kfc")
        s_u = sem("s_u")
        s_prod = sem("s_prod")
        s_spec = sem("s_spec")
        s_y = sem("s_y")
        s_stat = sem("s_stat")
        s_mv = sem("s_mv")
        s_sd = sem("s_sd")
        s_rstd = sem("s_rstd")
        s_ln = sem("s_ln")
        s_xt = sem("s_xt")
        s_xtc = sem("s_xtc")

        PAR = 2 + 2 + 4 + 3
        EDGE = [[bank[0], bank[1]], [bank[2], bank[3]]]
        UB = [[bank[4], bank[5]], [bank[6], bank[7]]]
        YB = [bank[0], bank[2]]
        XB = [bank[1], bank[3]]
        def args(eng, c):
            if c >= 2:
                eng.wait_ge(s_ksum, c - 1)
            cols = neg_dta[:, c * E_CH:(c + 1) * E_CH]
            eng.tensor_tensor(decay[:, c % 2], cols.unsqueeze(2).broadcast_to([P, E_CH, P]),
                              RAMP.unsqueeze(1).broadcast_to([P, E_CH, P]), ALU.mult).then_inc(s_arg[c % 2], 1)

        block = ctx.enter_context(nc.Block())

        @block.sync
        def _(sp):
            x, small_d, fwd_d, inv_d = A["x"], A["small_table"], A["fwd_table"], A["inv_table"]

            def load_image(b):
                if b >= NX:
                    sp.wait_ge(s_gray, b - NX + 1)
                sp.dma_start(image[:, b % NX], x[b].rearrange("c (q p) m -> p (c q) m", p=P)
                             ).then_inc(s_image[b % NX], 16)

            sp.dma_start(log_dt[0:64, :], A["log_dt"][0:MP].partition_broadcast(64)).then_inc(s_par, 16)
            sp.dma_start(log_dt[64:128, :], A["log_dt"][MP:M].partition_broadcast(64)).then_inc(s_par, 16)
            for half in range(2):
                sp.dma_start(a_log[64 * half:64 * half + 64, :],
                             A["A_log"].rearrange("(n a) -> n a", a=1)).then_inc(s_par, 16)
            load_image(0)
            load_image(1)
            sp.dma_start(keep["raw1"][:], A["W1"][E].rearrange("(c p) i -> p c i", p=P)).then_inc(keep["s_raw1"], 16)
            sp.dma_start(keep["raw2"][:], A["W2"][E].rearrange("(a p) c -> p a c", p=P)).then_inc(keep["s_raw2"], 16)
            for f in range(2):
                for k, dy in enumerate((2, 0)):
                    sp.dma_start(seam_taps[3 * k:3 * k + 3, f:f + 1],
                                 A["scharr"][f, 0, dy, :].rearrange("(n a) -> n a", a=1)).then_inc(s_par, 16)
            for b in range(2, B):
                load_image(b)
                if b % 2:
                    g = b // 2 - 1
                    sp.wait_ge(s_gray, 2 * g + 2)
                    for k, (p, lh) in enumerate(((0, 1), (P - 1, 0))):
                        for dx in range(3):
                            sp.dma_start(edge_rows[3 * k + dx:3 * k + dx + 1, 2 * g:2 * g + 2, :],
                                         gray[p:p + 1, lh, 2 * g:2 * g + 2, dx:dx + M]).then_inc(s_rows[g], 16)
            n = zero.shape[1]
            sp.wait_ge(s_pad, 4)
            for i in range(12):
                sp.dma_start(A["xs_d"].rearrange("(p r) c -> p (r c)", p=P)[:, i * n:(i + 1) * n], zero[:]
                             ).then_inc(keep["s_zero"], 16)
            g = PAIRS - 1
            sp.wait_ge(s_gray, 2 * g + 2)
            for k, (p, lh) in enumerate(((0, 1), (P - 1, 0))):
                for dx in range(3):
                    sp.dma_start(edge_rows[3 * k + dx:3 * k + dx + 1, 2 * g:2 * g + 2, :],
                                 gray[p:p + 1, lh, 2 * g:2 * g + 2, dx:dx + M]).then_inc(s_rows[g], 16)
            sp.wait_ge(keep["s_zero"], 12 * 16)

        @block.gpsimd
        def _(pool):
            pool.memset(gray[:, :, :, 0:1], 0.0).then_inc(s_pad, 1)
            pool.memset(gray[:, :, :, M + 1:M + 2], 0.0).then_inc(s_pad, 1)
            pool.memset(eps_t[:], EPS).then_inc(s_pad, 1)
            pool.memset(zero[:], 0.0).then_inc(s_pad, 1)
            pool.memset(c_decay[:], 0.0).then_inc(s_cz, 1)
            pool.wait_ge(s_const, 16)
            pool.wait_ge(s_dta, 1)
            for c in range(N_CH):
                if c % 2:
                    args(pool, c)

            def sum_filters(g):
                for lh in range(LH):
                    pool.wait_ge(s_abs, 4 * g + 2 * lh + 2)
                    pool.tensor_tensor(h[:, lh, g, :], half_abs[:, lh, 0, :], half_abs[:, lh, 1, :],
                                       ALU.add).then_inc(s_h, 1)

            def sum_products(g):
                for kc in range(KC):
                    pool.wait_ge(s_prod, 4 * (KC * g + kc) + 4)
                    if g >= 2:
                        pool.wait_ge(s_y, LH * (g - 1))
                    pool.tensor_tensor(spec[:, g % 2, kc, 0, :], prod[:, kc, 0, :], prod[:, kc, 1, :],
                                       ALU.subtract).then_inc(s_spec, 1)
                    pool.tensor_tensor(spec[:, g % 2, kc, 1, :], prod[:, kc, 2, :], prod[:, kc, 3, :],
                                       ALU.add).then_inc(s_spec, 1)

            for g in range(PAIRS):
                sum_filters(g)
                if g:
                    sum_products(g - 1)
            sum_products(PAIRS - 1)

        @block.scalar
        def _(act):
            act.dma_start(small[:], A["small_table"]).then_inc(s_const, 16)
            act.dma_start(taps[:].rearrange("p f y x -> p (f y x)"),
                          A["scharr"].rearrange("f a y x -> (f a y x)").partition_broadcast(P)).then_inc(s_par, 16)
            act.dma_start(c_in[:], A["C_re"].rearrange("(a p) n -> p a n", p=P)).then_inc(s_par, 16)
            act.dma_start(d_row[:], A["D"].rearrange("(a m) -> a m", a=1)).then_inc(s_par, 16)
            act.dma_start(fwd[:].rearrange("p a b c -> p (a b c)"), A["fwd_table"]).then_inc(s_dft, 16)
            act.dma_start(inv[:].rearrange("p a b c -> p (a b c)"), A["inv_table"]).then_inc(s_dft, 16)

            act.wait_ge(s_par, 16 * PAR)
            act.activation(a_exp[:], a_log[:], ACT.Exp).then_inc(s_exp0, 1)
            act.activation(dt_exp[:], log_dt[:], ACT.Exp).then_inc(s_exp0, 1)
            act.wait_ge(s_dta, 1)
            act.activation(far[:], neg_dta[:], ACT.Exp, scale=float(P)).then_inc(s_far, 1)

            def gray_first(b):
                act.wait_ge(s_image[b % NX], 16 * (b // NX + 1))
                act.activation(gray[:, :, b, 1:M + 1], image[:, b % NX, 0], ACT.Copy,
                               scale=GRAY[0]).then_inc(s_gray1, 1)

            def exps(c):
                act.wait_ge(s_arg[c % 2], c // 2 + 1)
                act.activation(decay[:, c % 2], decay[:, c % 2], ACT.Exp).then_inc(s_decay, 1)

            def abs_edges(g):
                for lh in range(LH):
                    for f in range(2):
                        act.wait_ge(s_edge, 4 * g + 2 * lh + f + 1)
                        if g:
                            act.wait_ge(s_h, LH * (g - 1) + lh + 1)
                        act.activation(half_abs[:, lh, f, :], EDGE[lh][f], ACT.Abs, scale=0.5).then_inc(s_abs, 1)

            def deviation(g):
                act.wait_ge(s_mv, 4 * g + 4)
                act.activation(sd[:, 4 * g:4 * g + 4], mv[:, 4 * g:4 * g + 4, 1], ACT.Sqrt,
                               bias=eps_t[:, 0:1]).then_inc(s_sd, 1)

            def copy_xt(g):
                for c in range(2):
                    act.wait_ge(s_xt, 2 * g + c + 1)
                    act.activation(xT[:, c, g * W2:(g + 1) * W2], XB[c], ACT.Copy).then_inc(s_xtc, 1)

            act.wait_ge(s_pad, 4)
            gray_first(0)
            gray_first(1)
            for c in range(N_CH):
                exps(c)
                if c == 3:
                    gray_first(2)
                    gray_first(3)
            abs_edges(0)
            gray_first(4)
            gray_first(5)
            act.wait_ge(s_ksum, N_CH)
            act.activation(taps_k[:].rearrange("p a h m -> p m h a"),
                           bank[7].rearrange("p (m h a) -> p m h a", h=2, a=LH), ACT.Copy).then_inc(s_kcopy, 1)
            for kc in range(KC):
                act.wait_ge(s_kf, kc + 1)
                act.activation(kf[:, 2 * kc:2 * kc + 2, :].rearrange("p a m -> p (a m)"), bank[4 + kc],
                               ACT.Copy).then_inc(s_kfc, 1)
            abs_edges(1)
            gray_first(6)
            gray_first(7)
            for g in range(2, PAIRS):
                deviation(g - 2)
                copy_xt(g - 2)
                abs_edges(g)
            for g in range(PAIRS - 2, PAIRS):
                deviation(g)
                copy_xt(g)

        @block.tensor
        def _(pe):
            pe.wait_ge(s_const, 16)
            pe.wait_ge(s_par, 16 * PAR)
            pe.transpose(bank[6][:, 0:P], c_in[:].rearrange("p a n -> p (a n)"), IDENT).then_inc(s_ct, 1)

            def edges(g):
                pe.wait_ge(s_gray, 2 * g + 2)
                pe.wait_ge(s_rows[g], 16 * 6)
                for lh in range(LH):
                    if g:
                        pe.wait_ge(s_abs, 4 * (g - 1) + 2 * lh + 2)
                    if g >= 2:
                        pe.wait_ge(s_ln, g - 1)
                        pe.wait_ge(s_xtc, 2 * (g - 1))
                    for f in range(2):
                        for dx in range(3):
                            pe.matmul(EDGE[lh][f], stencil[:, f, dx, :], gray[:, lh, 2 * g:2 * g + 2, dx:dx + M],
                                      start=(dx == 0), stop=False)
                        pe.matmul(EDGE[lh][f], seam[:, f, lh, :], edge_rows[:, 2 * g:2 * g + 2, :],
                                  start=False, stop=True).then_inc(s_edge, 1)

            def spectra(g):
                pe.wait_ge(s_h, LH * (g + 1))
                for kc in range(KC):
                    if g:
                        pe.wait_ge(s_prod, 4 * (KC * (g - 1) + kc) + 4)
                    else:
                        pe.wait_ge(s_kfc, KC)
                    for ri in range(2):
                        for lh in range(LH):
                            mm = pe.matmul(UB[kc][ri], fwd[:, lh, 2 * kc + ri, :], h[:, lh, g, :],
                                           start=(lh == 0), stop=(lh == LH - 1))
                    mm.then_inc(s_u, 1)

            def convolved(g):
                pe.wait_ge(s_spec, 4 * (g + 1))
                if g + 1 < PAIRS:
                    pe.wait_ge(s_abs, 4 * (g + 2))
                else:
                    pe.wait_ge(s_ln, g)
                for lh in range(LH):
                    for kc in range(KC):
                        for ri in range(2):
                            mm = pe.matmul(YB[lh], inv[:, kc, ri, lh * P:(lh + 1) * P], spec[:, g % 2, kc, ri, :],
                                           start=(kc == 0 and ri == 0), stop=(kc == KC - 1 and ri == 1))
                    mm.then_inc(s_y, 1)

            def transposes(g):
                pe.wait_ge(s_ln, g + 1)
                for c in range(2):
                    if g == PAIRS - 1:
                        pe.wait_ge(s_xtc, 2 * g)
                    for t in range(4):
                        mm = pe.transpose(XB[c][:, t * P:(t + 1) * P],
                                          hln[:, 4 * g + t, c * P:(c + 1) * P], IDENT)
                    mm.then_inc(s_xt, 1)

            pe.wait_ge(s_stencil, 2 * 2 * 3 - 6 + 4)
            edges(0)
            pe.wait_ge(s_cd, 4)
            for c in range(N_CH):
                pe.wait_ge(s_decay, c + 1)
                for m in range(E_CH):
                    mp = c * E_CH + m
                    mm = pe.matmul(bank[7][:, 4 * mp:4 * mp + 4], decay[:, c % 2, m, :],
                                   c_decay[:, mp].rearrange("p a b -> p (a b)"), start=True, stop=True)
                mm.then_inc(s_ksum, 1)
            pe.wait_ge(s_kd, 1)
            pe.wait_ge(s_dft, 32)
            for kc in range(KC):
                for ri in range(2):
                    for lh in range(LH):
                        mm = pe.matmul(bank[4 + kc][:, ri * M:(ri + 1) * M], fwd[:, lh, 2 * kc + ri, :],
                                       taps_k[:, lh].rearrange("p h m -> p (h m)"),
                                       start=(lh == 0), stop=(lh == LH - 1))
                mm.then_inc(s_kf, 1)
            spectra(0)
            edges(1)
            convolved(0)
            spectra(1)
            transposes(0)
            for g in range(2, PAIRS):
                edges(g)
                convolved(g - 1)
                spectra(g)
                transposes(g - 1)
            convolved(PAIRS - 1)
            transposes(PAIRS - 1)

        @block.vector
        def _(dve):
            dve.wait_ge(s_exp0, 2)
            dve.tensor_scalar(neg_dta[:], dt_exp[:], a_exp[:, 0:1], -1.0, ALU.mult, ALU.mult).then_inc(s_dta, 1)
            dve.wait_ge(s_const, 16)
            dve.wait_ge(s_par, 16 * PAR)
            for dy in range(3):
                if dy:
                    dve.wait_ge(s_st0, 6 * dy)
                for f in range(2):
                    for dx in range(3):
                        tap = taps[:, f, dy, dx:dx + 1]
                        if dy == 0:
                            st = dve.tensor_scalar(stencil[:, f, dx, :], BAND[0], tap, None, ALU.mult)
                        else:
                            st = dve.scalar_tensor_tensor(stencil[:, f, dx, :], BAND[dy], tap,
                                                          stencil[:, f, dx, :], ALU.mult, ALU.add)
                        st.then_inc(s_st0 if dy < 2 else s_stencil, 1)
            for f in range(2):
                for lh in range(LH):
                    dve.tensor_scalar(seam[:, f, lh, :], SEAM[lh], seam_taps[:, f:f + 1], None,
                                      ALU.mult).then_inc(s_stencil, 1)

            def gray_rest(b):
                dve.wait_ge(s_gray1, b + 1)
                for c in (1, 2):
                    if c == 2:
                        dve.wait_ge(s_gray2, b + 1)
                    dve.scalar_tensor_tensor(gray[:, :, b, 1:M + 1], image[:, b % NX, c], GRAY[c],
                                             gray[:, :, b, 1:M + 1], ALU.mult, ALU.add
                                             ).then_inc(s_gray2 if c == 1 else s_gray, 1)

            dve.wait_ge(s_dta, 1)
            args(dve, 0)
            gray_rest(0)
            gray_rest(1)
            dve.wait_ge(s_ct, 1)
            dve.wait_ge(s_cz, 1)
            dve.wait_ge(s_far, 1)
            for mh in range(2):
                r = slice(64 * mh, 64 * mh + 64)
                dve.tensor_copy(c_decay[r, :, mh, 0], bank[6][r, 0:P]).then_inc(s_cd, 1)
                dve.tensor_tensor(c_decay[r, :, mh, 1], bank[6][r, 0:P], far[r, :], ALU.mult).then_inc(s_cd, 1)
            for c in range(2, N_CH, 2):
                args(dve, c)
                if c == 4:
                    gray_rest(2)
                    gray_rest(3)
            dve.wait_ge(s_kcopy, 1)
            dve.scalar_tensor_tensor(taps_k[0:1, 0].rearrange("p h m -> p (h m)"), d_row[:], 1.0,
                                     taps_k[0:1, 0].rearrange("p h m -> p (h m)"), ALU.add, ALU.add
                                     ).then_inc(s_kd, 1)
            gray_rest(4)
            gray_rest(5)

            def products(g):
                for kc in range(KC):
                    dve.wait_ge(s_u, KC * g + kc + 1)
                    if g:
                        dve.wait_ge(s_spec, 4 * (g - 1) + 2 * kc + 2)
                    for n, (u, k) in enumerate(((0, 0), (1, 1), (0, 1), (1, 0))):
                        dve.tensor_tensor(prod[:, kc, n, :].rearrange("p (b m) -> p b m", b=2),
                                          UB[kc][u].rearrange("p (b m) -> p b m", b=2),
                                          kf[:, 2 * kc + k, :].unsqueeze(1).broadcast_to([P, 2, M]),
                                          ALU.mult).then_inc(s_prod, 1)

            def layernorm(g):
                for lh in range(LH):
                    dve.wait_ge(s_y, LH * g + lh + 1)
                    for b in range(2):
                        t = 4 * g + 2 * b + lh
                        dve.bn_stats(stats[:, t, :], YB[lh][:, b * M:(b + 1) * M]).then_inc(s_stat, 1)
                dve.wait_ge(s_stat, 4 * g + 4)
                for t in range(4 * g, 4 * g + 4):
                    dve.bn_aggr(mv[:, t, :], stats[:, t, :]).then_inc(s_mv, 1)
                dve.wait_ge(s_sd, g + 1)
                dve.reciprocal(rstd[:, 4 * g:4 * g + 4], sd[:, 4 * g:4 * g + 4]).then_inc(s_rstd, 1)
                dve.wait_ge(s_rstd, g + 1)
                for lh in range(LH):
                    for b in range(2):
                        t = 4 * g + 2 * b + lh
                        ts = dve.tensor_scalar(hln[:, t, :], YB[lh][:, b * M:(b + 1) * M], mv[:, t, 0:1],
                                               rstd[:, t:t + 1], ALU.subtract, ALU.mult)
                ts.then_inc(s_ln, 1)

            dve.wait_ge(s_kfc, KC)
            products(0)
            gray_rest(6)
            gray_rest(7)
            for g in range(1, PAIRS):
                layernorm(g - 1)
                products(g)
            layernorm(PAIRS - 1)


def experts(nc, A, keep, out):
    hln, xT, small, eps_t, bank = (keep[k] for k in ("hln", "xT", "small", "eps", "bank"))
    raw1, raw2, s_raw1, s_raw2 = (keep[k] for k in ("raw1", "raw2", "s_raw1", "s_raw2"))
    BEFORE, ONES, RAMP = small[:, 4 * P:5 * P], small[:, 5 * P:6 * P], small[:, 6 * P:7 * P]
    IDENT = small[:, 3 * P:4 * P]
    UPTO = small[:, 9 * P:9 * P + E * E].rearrange("p (e f) -> p e f", f=E)
    with ExitStack() as ctx:
        def sb(name, shape, dt=F32):
            return ctx.enter_context(nc.sbuf_tensor(name, shape, dt))

        def sem(name):
            return ctx.enter_context(nc.semaphore(name))

        wr1 = sb("wr1", [P, 2, R1])
        br1 = sb("br1", [R1, 1])
        wr2 = sb("wr2", [R1, E])
        br2 = sb("br2", [P, E])
        b1_in = sb("b1_in", [(E + 1) * IC, P])
        b1T = sb("b1T", [P, (E + 1) * IC])
        b1_now = sb("b1_now", [P, 2, IC])
        b2_rows = sb("b2_rows", [P, E + 1, M])
        w1_hi, w1_lo = sb("w1_hi", [P, 2, 2, I], F32R), sb("w1_lo", [P, 2, 2, I], F32R)
        w2_hi, w2_lo = sb("w2_hi", [P, 2, IC, M], F32R), sb("w2_lo", [P, 2, IC, M], F32R)
        x_hi, x_lo = sb("x_hi", [P, 2, 2, T], F32R), sb("x_lo", [P, 2, 2, T], F32R)
        h1 = sb("h1", [P, IC, T])
        r1T = h1[0:R1].rearrange("p a t -> p (a t)")
        rows = h1[:].rearrange("p a t -> p (a t)").rearrange("p (n m) -> p n m", m=M)
        h1_hi, h1_lo = sb("h1_hi", [P, 2, IC, T], F32R), sb("h1_lo", [P, 2, IC, T], F32R)
        xs = sb("xs", [P, 2, 2, M])
        acc = sb("acc", [P, TILES, M])
        y = sb("y", [P, 2, 2, M])

        def rt(name, shape=(P, TILES, E), dt=F32):
            return sb(name, list(shape), dt)
        logit, eq, key, rank = rt("logit"), rt("eq"), rt("key"), rt("rank")
        pick = [rt("pick0"), rt("pick1")]
        best = [rt("best0", (P, TILES)), rt("best1", (P, TILES))]
        both = rt("both")
        col, col2 = rt("col", (P, TILES)), rt("col2", (P, TILES))
        gate_w = rt("gate_w", (P, 2, TILES))
        rev = rt("rev", (P, E))
        n_exp, slots_e, end_e, base_e = (rt(n, (P, E)) for n in ("n_exp", "slots_e", "end_e", "base_e"))
        cmp = rt("cmp", (P, max(SLOTS, E), E))
        pos = rt("pos", (P, 2, TILES), I32)
        slot_f = rt("slot_f", (P, SLOTS))
        slot_e = rt("slot_e", (P, SLOTS), I32)
        stats, mv = sb("stats2", [P, TILES, 6]), sb("mv2", [P, TILES, 2])
        sd, rstd = sb("sd2", [P, TILES]), sb("rstd2", [P, TILES])

        s_par = sem("s_par2")
        s_r1 = sem("s_r1")
        s_relu = sem("s_relu")
        s_logit = sem("s_logit")
        s_b1t, s_b1c = sem("s_b1t"), sem("s_b1c")
        s_soft = sem("s_soft")
        s_ro = sem("s_ro")
        s_picked = sem("s_picked")
        s_rank = sem("s_rank")
        s_pos = sem("s_pos")
        s_acc0 = sem("s_acc0")
        s_scat = sem("s_scat")
        s_w1h, s_w1l, s_w2h, s_w2l = sem("s_w1h"), sem("s_w1l"), sem("s_w2h"), sem("s_w2l")
        s_xs = [sem("s_xs0"), sem("s_xs1")]
        s_xt, s_xh, s_xl = sem("s_xt2"), sem("s_xh"), sem("s_xl")
        s_bias = sem("s_bias")
        s_g1, s_silu, s_hhi, s_hlo, s_g2 = sem("s_g1"), sem("s_silu"), sem("s_hhi"), sem("s_hlo"), sem("s_g2")
        s_y = sem("s_y2")
        s_store = [sem("s_store0"), sem("s_store1")]
        s_rows = [sem(f"s_rows2_{i}") for i in range(GR)]
        s_mix, s_used = sem("s_mix"), sem("s_used")
        s_st, s_mv, s_sd, s_rstd, s_fin = sem("s_st2"), sem("s_mv2"), sem("s_sd2"), sem("s_rstd2"), sem("s_fin")
        s_out = sem("s_out")

        G2 = [bank[4], bank[5]]
        XB, RB = bank[6], bank[7]
        xs_d, ys_d = A["xs_d"], A["ys_d"]
        NPAR = 5
        block = ctx.enter_context(nc.Block())

        @block.sync
        def _(sp):
            def load_w1(v, e):
                sp.wait_ge(s_w1l, v)
                sp.dma_start(raw1[:], A["W1"][e].rearrange("(c p) i -> p c i", p=P)).then_inc(s_raw1, 16)

            def load_w2(v, e):
                sp.wait_ge(s_w2l, v)
                sp.dma_start(raw2[:], A["W2"][e].rearrange("(a p) c -> p a c", p=P)).then_inc(s_raw2, 16)

            def load_x(s, par, first=False):
                if not first:
                    sp.wait_ge(s_xt, s - 1)
                sp.dma_start(xs[:, par], xs_d[bass.ds(s * T, T), :].rearrange("(j p) c -> p j c", p=P)
                             ).then_inc(s_xs[par], 16)

            def store_y(s, par):
                sp.wait_ge(s_y, SHARED + s + 1)
                sp.dma_start(ys_d[bass.ds(s * T, T), :].rearrange("(j p) c -> p j c", p=P), y[:, par]
                             ).then_inc(s_store[par], 16)

            def expert_of(s):
                return sp.value_load(slot_e[0:1, bass.ds(s, 1)], min_val=0, max_val=E - 1)

            def slot(s, par, static=True):
                if not static or s + 1 < SLOTS:
                    load_w1(s + 2, expert_of(s + 1))
                    load_x(s + 1, 1 - par, first=static and s == 0)
                load_w2(s + 1, expert_of(s))
                if not static or s >= 2:
                    store_y(s - 2, par)

            sp.wait_ge(s_pos, 1)
            load_w1(1, expert_of(0))
            sp.wait_ge(s_scat, 16 * 2 * TILES)
            load_x(0, 0, first=True)
            slot(0, 0)
            slot(1, 1)
            with sp.Fori(2, SLOTS - 3, 2) as s:
                slot(s, 0, static=False)
                slot(s + 1, 1, static=False)
            for s in range(SLOTS - 2, SLOTS):
                slot(s, s % 2)
            store_y(SLOTS - 2, 0)
            store_y(SLOTS - 1, 1)
            for q in range(4):
                sp.wait_ge(s_fin, q + 1)
                sp.dma_start(out[2 * q:2 * q + 2].rearrange("b (h p) m -> p (b h) m", p=P),
                             acc[:, 4 * q:4 * q + 4, :]).then_inc(s_out, 16)
            sp.wait_ge(s_out, 64)

        @block.gpsimd
        def _(pool):
            pool.wait_ge(s_par, 16 * NPAR)
            for t in range(0, TILES, 4):
                pool.tensor_tensor(acc[:, t:t + 4, :], hln[:, t:t + 4, :],
                                   b2_rows[:, E:E + 1, :].broadcast_to([P, 4, M]), ALU.add).then_inc(s_acc0, 1)
            pool.wait_ge(s_pos, 1)
            for t in range(TILES):
                for k in range(2):
                    pool.indirect_dma_start(xs_d, bass.IndirectOffsetOnAxis(ap=pos[:, k, t:t + 1].bitcast(U32), axis=0),
                                            hln[:, t, :], None).then_inc(s_scat, 16)

            def lo(u, par):
                for j in range(PAIRS1):
                    pool.wait_ge(s_hhi, PAIRS1 * u + j + 1)
                    pool.tensor_tensor(h1_lo[:, par, 2 * j:2 * j + 2, :], h1[:, 2 * j:2 * j + 2, :],
                                       h1_hi[:, par, 2 * j:2 * j + 2, :].bitcast(F32), ALU.subtract).then_inc(s_hlo, 1)

            with pool.Fori(SHARED, SHARED + SLOTS - 1, 2) as u:
                lo(u, 0)
                lo(u + 1, 1)
            for par in range(2):
                pool.wait_ge(s_store[par], 16 * (SLOTS // 2))
            for n in range(2 * TILES):
                if n >= GR:
                    pool.wait_ge(s_mix, n - GR + 1)
                pool.indirect_dma_start(rows[:, n % GR, :], None, ys_d,
                                        bass.IndirectOffsetOnAxis(ap=pos[:, n % 2, n // 2:n // 2 + 1].bitcast(U32), axis=0)
                                        ).then_inc(s_rows[n % GR], 16)

        @block.scalar
        def _(act):
            act.dma_start(wr1[:], A["Wr1"].rearrange("(c p) r -> p c r", p=P)).then_inc(s_par, 16)
            act.dma_start(br1[:], A["br1"].rearrange("(r a) -> r a", a=1)).then_inc(s_par, 16)
            act.dma_start(wr2[:], A["Wr2"]).then_inc(s_par, 16)
            act.dma_start(br2[:], A["br2"].partition_broadcast(P)).then_inc(s_par, 16)
            act.dma_start(b2_rows[:].rearrange("p e m -> p (e m)"),
                          A["b2"].rearrange("e m -> (e m)").partition_broadcast(P)).then_inc(s_par, 16)
            act.dma_start(b1_in[:], A["b1"].rearrange("e (a p) -> (e a) p", p=P)).then_inc(s_b1t, 16)

            def w1h(v, par, first=False):
                act.wait_ge(s_raw1, 16 * v + 16)
                if not first:
                    act.wait_ge(s_g1, PAIRS1 * (v + SHARED - 2))
                act.activation(w1_hi[:, par], raw1[:], ACT.Copy).then_inc(s_w1h, 1)

            def w2h(v, par, first=False):
                act.wait_ge(s_raw2, 16 * v + 16)
                if not first:
                    act.wait_ge(s_g2, v + SHARED - 2)
                act.activation(w2_hi[:, par], raw2[:], ACT.Copy).then_inc(s_w2h, 1)

            def xh(u, par, shared, first=False):
                if not first:
                    act.wait_ge(s_g1, PAIRS1 * (u - 1))
                if shared:
                    src = xT[:, :, bass.ds(u * T, T)]
                else:
                    act.wait_ge(s_xt, u - SHARED + 1)
                    src = XB.rearrange("p (c t) -> p c t", c=2)
                act.activation(x_hi[:, par], src, ACT.Copy).then_inc(s_xh, 1)

            def silu(u, par, pairs, bias, shared, first=False):
                for j in pairs:
                    act.wait_ge(s_g1, PAIRS1 * u + j + 1)
                    if not first:
                        act.wait_ge(s_hlo, PAIRS1 * (u - 1) + j + 1)
                    for a in range(2):
                        ic = 2 * j + a
                        ins = act.activation(h1[:, ic, :], bank[j][:, a * T:(a + 1) * T], ACT.Silu,
                                             bias=bias[:, ic:ic + 1])
                    ins.then_inc(s_silu, 1)
                    if shared:
                        act.wait_ge(s_silu, PAIRS1 * u + j + 1)
                        act.activation(h1_hi[:, par, 2 * j:2 * j + 2, :], h1[:, 2 * j:2 * j + 2, :], ACT.Copy
                                       ).then_inc(s_hhi, 1)

            def shared_unit(u, par, first=False):
                b = b1T[:, E * IC:(E + 1) * IC]
                if not first:
                    act.wait_ge(s_g2, u - 1)
                silu(u, par, range(PAIRS1), b, True, first)

            def slot(u, par, last=False):
                s = u - SHARED
                e = act.value_load(slot_e[0:1, bass.ds(s, 1)], min_val=0, max_val=E - 1)
                act.activation(b1_now[:, par, :], b1T[:, bass.ds(e * IC, IC)], ACT.Copy).then_inc(s_bias, 1)
                act.wait_ge(s_bias, s + 1)
                silu(u, par, (0, 1), b1_now[:, par, :], False)
                if not last:
                    w1h(s + 2, par)
                silu(u, par, (2, 3), b1_now[:, par, :], False)
                if not last:
                    xh(u + 1, 1 - par, False)
                w2h(s + 1, 1 - par)

            act.wait_ge(s_par, 16 * NPAR)
            for g in range(PAIRS):
                act.wait_ge(s_r1, g + 1)
                act.activation(r1T[:, g * W2:(g + 1) * W2], bank[g][0:R1, :], ACT.Relu,
                               bias=br1[:, 0:1]).then_inc(s_relu, 1)
            w1h(0, 0, first=True)
            xh(0, 0, True, first=True)
            xh(1, 1, True, first=True)
            act.wait_ge(s_b1t, 17)
            act.activation(b1T[:], XB[:, 0:(E + 1) * IC], ACT.Copy).then_inc(s_b1c, 1)
            w2h(0, 0, first=True)
            act.wait_ge(s_ro, SOFT)
            act.activation(logit[:], logit[:], ACT.Exp).then_inc(s_soft, 1)
            act.wait_ge(s_ro, SOFT2)
            act.activation(col2[:], col2[:], ACT.Exp, scale=0.5).then_inc(s_soft, 1)
            act.wait_ge(s_pos, 1)
            act.wait_ge(s_b1c, 1)
            shared_unit(0, 0, first=True)
            with act.Fori(1, SHARED - 2, 2) as u:
                shared_unit(u, 1)
                xh(u + 1, 0, True)
                shared_unit(u + 1, 0)
                xh(u + 2, 1, True)
            shared_unit(SHARED - 1, 1)
            w1h(1, 1, first=True)
            xh(SHARED, 0, False)
            with act.Fori(SHARED, SHARED + SLOTS - 3, 2) as u:
                slot(u, 0)
                slot(u + 1, 1)
            slot(SHARED + SLOTS - 2, 0)
            slot(SHARED + SLOTS - 1, 1, last=True)
            for q in range(4):
                act.wait_ge(s_mv, 4 * q + 4)
                act.activation(sd[:, 4 * q:4 * q + 4], mv[:, 4 * q:4 * q + 4, 1], ACT.Sqrt,
                               bias=eps_t[:, 0:1]).then_inc(s_sd, 1)

        @block.tensor
        def _(pe):
            def g1(u, par, wpar, version, first=False):
                pe.wait_ge(s_w1l, version + 1)
                pe.wait_ge(s_xl, u + 1)
                for j in range(PAIRS1):
                    if not first:
                        pe.wait_ge(s_silu, PAIRS1 * (u - 1) + j + 1)
                    for a in range(2):
                        i0 = (2 * j + a) * P
                        parts = [(w, x) for w, x in ((w1_hi, x_hi), (w1_hi, x_lo), (w1_lo, x_hi))]
                        for n, (w, x) in enumerate(parts):
                            for c in range(2):
                                mm = pe.matmul(bank[j][:, a * T:(a + 1) * T], w[:, wpar, c, i0:i0 + P],
                                               x[:, par, c, :], start=(n == 0 and c == 0), stop=(n == 2 and c == 1))
                    mm.then_inc(s_g1, 1)

            def g2(u, par, wpar, version, first=False):
                pe.wait_ge(s_w2l, version + 1)
                if not first:
                    pe.wait_ge(s_y, u - 1)
                pe.wait_ge(s_hlo, PAIRS1 * u + PAIRS1)
                for j in range(2):
                    for ic in range(IC):
                        for n, (h, w) in enumerate(((h1_hi, w2_hi), (h1_hi, w2_lo), (h1_lo, w2_hi))):
                            mm = pe.matmul(G2[par][:, j * M:(j + 1) * M], h[:, par, ic, j * P:(j + 1) * P],
                                           w[:, wpar, ic, :], start=(ic == 0 and n == 0), stop=(ic == IC - 1 and n == 2))
                mm.then_inc(s_g2, 1)

            def transposes(s, par, count, first=False):
                pe.wait_ge(s_xs[par], count)
                if not first:
                    pe.wait_ge(s_xl, SHARED + s)
                for c in range(2):
                    for j in range(2):
                        mm = pe.transpose(XB[:, c * T + j * P:c * T + (j + 1) * P],
                                          xs[:, par, j, c * P:(c + 1) * P], IDENT)
                mm.then_inc(s_xt, 1)

            def slot(s, par, static=True):
                g1(SHARED + s, par, 1 - par, s + 1)
                if not static or s + 1 < SLOTS:
                    transposes(s + 1, 1 - par, 8 * s + (16 if par == 0 else 24))
                if static and s == 0:
                    g2(SHARED - 1, 1, 0, 0)
                else:
                    g2(SHARED + s - 1, 1 - par, par, s)

            pe.wait_ge(s_par, 16 * NPAR)
            for g in range(PAIRS):
                for c in range(2):
                    mm = pe.matmul(bank[g][0:R1, :], wr1[:, c, :], xT[:, c, g * W2:(g + 1) * W2],
                                   start=(c == 0), stop=(c == 1))
                mm.then_inc(s_r1, 1)
            pe.wait_ge(s_b1t, 16)
            pe.transpose(XB[:, 0:(E + 1) * IC], b1_in[:], IDENT[0:(E + 1) * IC, 0:(E + 1) * IC]).then_inc(s_b1t, 1)
            pe.wait_ge(s_relu, PAIRS)
            for t in range(TILES):
                mm = pe.matmul(RB[:, t * E:(t + 1) * E], r1T[:, t * P:(t + 1) * P], wr2[:], start=True, stop=True)
            mm.then_inc(s_logit, 1)
            g1(0, 0, 0, 0, first=True)
            pe.wait_ge(s_picked, 1)
            pe.matmul(RB[:, 128:256], BEFORE, both[:].rearrange("p t e -> p (t e)"), start=True, stop=False)
            for t in range(TILES - 1):
                n = TILES - 1 - t
                pe.matmul(RB[:, 128 + (t + 1) * E:256], ONES, both[:, t:t + 1, :].broadcast_to([P, n, E]),
                          start=False, stop=(t == TILES - 2))
            pe.matmul(RB[:, 256:256 + E], ONES, n_exp[:], start=True, stop=True).then_inc(s_rank, 1)
            g1(1, 1, 0, 0)
            g2(0, 0, 0, 0, first=True)
            g1(2, 0, 0, 0)
            g2(1, 1, 0, 0, first=True)
            with pe.Fori(3, SHARED - 2, 2) as u:
                g1(u, 1, 0, 0)
                g2(u - 1, 0, 0, 0)
                g1(u + 1, 0, 0, 0)
                g2(u, 1, 0, 0)
            g1(SHARED - 1, 1, 0, 0)
            transposes(0, 0, 16, first=True)
            g2(SHARED - 2, 0, 0, 0)
            slot(0, 0)
            slot(1, 1)
            with pe.Fori(2, SLOTS - 3, 2) as s:
                slot(s, 0, static=False)
                slot(s + 1, 1, static=False)
            slot(SLOTS - 2, 0)
            slot(SLOTS - 1, 1)
            g2(SHARED + SLOTS - 1, 1, 0, SLOTS)

        @block.vector
        def _(dve):
            done = [0]

            def step(ins):
                done[0] += 1
                ins.then_inc(s_ro, 1)
                dve.wait_ge(s_ro, done[0])

            def w1l(v, par):
                dve.wait_ge(s_w1h, v + 1)
                dve.tensor_tensor(w1_lo[:, par], raw1[:], w1_hi[:, par].bitcast(F32), ALU.subtract).then_inc(s_w1l, 1)

            def w2l(v, par):
                dve.wait_ge(s_w2h, v + 1)
                dve.tensor_tensor(w2_lo[:, par], raw2[:], w2_hi[:, par].bitcast(F32), ALU.subtract).then_inc(s_w2l, 1)

            def xl(u, par, shared):
                dve.wait_ge(s_xh, u + 1)
                src = xT[:, :, bass.ds(u * T, T)] if shared else XB.rearrange("p (c t) -> p c t", c=2)
                dve.tensor_tensor(x_lo[:, par], src, x_hi[:, par].bitcast(F32), ALU.subtract).then_inc(s_xl, 1)

            def h1l(u, par, pairs):
                for j in pairs:
                    dve.wait_ge(s_hhi, PAIRS1 * u + j + 1)
                    dve.tensor_tensor(h1_lo[:, par, 2 * j:2 * j + 2, :], h1[:, 2 * j:2 * j + 2, :],
                                      h1_hi[:, par, 2 * j:2 * j + 2, :].bitcast(F32), ALU.subtract).then_inc(s_hlo, 1)

            def h1h(u, par, pairs):
                dve.wait_ge(s_g2, u - 1)
                for j in pairs:
                    dve.wait_ge(s_silu, PAIRS1 * u + j + 1)
                    dve.tensor_copy(h1_hi[:, par, 2 * j:2 * j + 2, :], h1[:, 2 * j:2 * j + 2, :]).then_inc(s_hhi, 1)

            def y_shared(u, par):
                dve.wait_ge(s_g2, u + 1)
                dve.tensor_tensor(acc[:, bass.ds(2 * u, 2), :], G2[par].rearrange("p (j c) -> p j c", j=2),
                                  acc[:, bass.ds(2 * u, 2), :], ALU.add).then_inc(s_y, 1)

            def y_slot(s, par, first=False):
                dve.wait_ge(s_g2, SHARED + s + 1)
                if not first:
                    dve.wait_ge(s_store[par], 8 * s - 8 * par)
                e = dve.value_load(slot_e[0:1, bass.ds(s, 1)], min_val=0, max_val=E - 1)
                dve.tensor_tensor(y[:, par], G2[par].rearrange("p (j c) -> p j c", j=2),
                                  b2_rows[:, bass.ds(e, 1), :].broadcast_to([P, 2, M]), ALU.add).then_inc(s_y, 1)

            def slot(s, par, static=True):
                if static and s < 2:
                    y_shared(SHARED + s - 2, par)
                else:
                    y_slot(s - 2, par, first=static and s < 4)
                h1h(SHARED + s, par, (0, 1))
                last = static and s == SLOTS - 1
                if not last:
                    w1l(s + 2, par)
                h1h(SHARED + s, par, (2, 3))
                if not last:
                    xl(SHARED + s + 1, 1 - par, False)
                w2l(s + 1, 1 - par)

            def over(ap, n):
                return ap.unsqueeze(2).broadcast_to([P, TILES, n])

            def tiles_of(ap):
                return ap.unsqueeze(1).broadcast_to([P, TILES, E])

            w1l(0, 0)
            xl(0, 0, True)
            xl(1, 1, True)
            dve.wait_ge(s_par, 16 * NPAR)
            dve.wait_ge(s_logit, 1)
            step(dve.tensor_tensor(logit[:], RB[:, 0:128].rearrange("p (t e) -> p t e", e=E), tiles_of(br2[:]), ALU.add))
            step(dve.tensor_scalar(rev[:], RAMP[:, 0:E], -1.0, float(E), ALU.mult, ALU.add))
            step(dve.tensor_reduce(col[:], logit[:], X, ALU.max))
            step(dve.tensor_tensor(logit[:], logit[:], over(col[:], E), ALU.subtract))
            assert done[0] == SOFT
            dve.wait_ge(s_soft, 1)
            step(dve.tensor_reduce(col[:], logit[:], X, ALU.add))
            step(dve.reciprocal(col2[:], col[:]))
            step(dve.tensor_tensor(logit[:], logit[:], over(col2[:], E), ALU.mult))
            for k in range(2):
                step(dve.tensor_reduce(best[k][:], logit[:], X, ALU.max))
                step(dve.tensor_tensor(eq[:], logit[:], over(best[k][:], E), ALU.is_equal))
                step(dve.tensor_tensor(key[:], eq[:], tiles_of(rev[:]), ALU.mult))
                step(dve.tensor_reduce(col[:], key[:], X, ALU.max))
                step(dve.tensor_tensor(pick[k][:], key[:], over(col[:], E), ALU.is_equal))
                if k == 0:
                    step(dve.scalar_tensor_tensor(logit[:], pick[0][:], -2.0, logit[:], ALU.mult, ALU.add))
            step(dve.tensor_tensor(both[:], pick[0][:], pick[1][:], ALU.add))
            step(dve.tensor_reduce(n_exp[:], both[:].rearrange("p t e -> p e t"), X, ALU.add))
            dve.engine_nop().then_inc(s_picked, 1)
            step(dve.tensor_tensor(col2[:], best[1][:], best[0][:], ALU.subtract))
            assert done[0] == SOFT2
            dve.wait_ge(s_soft, 2)
            step(dve.tensor_scalar(col[:], col2[:], 1.0, None, ALU.add))
            step(dve.reciprocal(gate_w[:, 0, :], col[:]))
            step(dve.tensor_tensor(gate_w[:, 1, :], col2[:], gate_w[:, 0, :], ALU.mult))
            dve.wait_ge(s_rank, 1)
            step(dve.tensor_copy(n_exp[:], RB[:, 256:256 + E]))
            step(dve.tensor_scalar(end_e[:], RAMP[:, 0:E], float(T), None, ALU.mult))
            step(dve.tensor_tensor(cmp[:, 0:E, :], n_exp[:].unsqueeze(2).broadcast_to([P, E, E]),
                                   end_e[:].unsqueeze(1).broadcast_to([P, E, E]), ALU.is_gt))
            step(dve.tensor_reduce(slots_e[:], cmp[:, 0:E, :], X, ALU.add))
            step(dve.tensor_tensor(cmp[:, 0:E, :], UPTO, slots_e[:].unsqueeze(1).broadcast_to([P, E, E]), ALU.mult))
            step(dve.tensor_reduce(end_e[:], cmp[:, 0:E, :], X, ALU.add))
            step(dve.tensor_tensor(base_e[:], end_e[:], slots_e[:], ALU.subtract))
            step(dve.tensor_scalar(base_e[:], base_e[:], float(T), None, ALU.mult))
            step(dve.tensor_tensor(rank[:], RB[:, 128:256].rearrange("p (t e) -> p t e", e=E), tiles_of(base_e[:]), ALU.add))
            for k in range(2):
                step(dve.tensor_tensor(key[:], rank[:], pick[k][:], ALU.mult))
                step(dve.tensor_reduce(col[:], key[:], X, ALU.add))
                step(dve.tensor_copy(pos[:, k, :], col[:]))
            step(dve.tensor_tensor(cmp[:, 0:SLOTS, :], end_e[:].unsqueeze(1).broadcast_to([P, SLOTS, E]),
                                   RAMP[:, 0:SLOTS].unsqueeze(2).broadcast_to([P, SLOTS, E]), ALU.is_le))
            step(dve.tensor_reduce(slot_f[:], cmp[:, 0:SLOTS, :], X, ALU.add))
            step(dve.tensor_scalar(slot_f[:], slot_f[:], float(E - 1), None, ALU.min))
            dve.tensor_copy(slot_e[:], slot_f[:]).then_inc(s_pos, 1)

            dve.wait_ge(s_acc0, 4)
            h1l(0, 0, range(PAIRS1))
            w2l(0, 0)
            h1l(1, 1, range(PAIRS1))
            xl(2, 0, True)
            y_shared(0, 0)
            h1l(2, 0, range(PAIRS1))
            xl(3, 1, True)
            with dve.Fori(3, SHARED - 2, 2) as u:
                y_shared(u - 2, 1)
                h1l(u, 1, range(PAIRS1))
                xl(u + 1, 0, True)
                y_shared(u - 1, 0)
                h1l(u + 1, 0, range(PAIRS1))
                xl(u + 2, 1, True)
            y_shared(SHARED - 3, 1)
            h1l(SHARED - 1, 1, range(PAIRS1))
            w1l(1, 1)
            xl(SHARED, 0, False)
            for s in range(4):
                slot(s, s % 2)
            with dve.Fori(4, SLOTS - 3, 2) as s:
                slot(s, 0, static=False)
                slot(s + 1, 1, static=False)
            for s in range(SLOTS - 2, SLOTS):
                slot(s, s % 2)
            y_slot(SLOTS - 2, 0)
            y_slot(SLOTS - 1, 1)

            for q in range(4):
                for t in range(4 * q, 4 * q + 4):
                    for k in range(2):
                        n = 2 * t + k
                        dve.wait_ge(s_rows[n % GR], 16 * (n // GR + 1))
                        if k:
                            dve.wait_ge(s_mix, n)
                        dve.scalar_tensor_tensor(acc[:, t, :], rows[:, n % GR, :], gate_w[:, k, t:t + 1],
                                                 acc[:, t, :], ALU.mult, ALU.add).then_inc(s_mix, 1)
                for t in range(4 * q, 4 * q + 4):
                    dve.wait_ge(s_mix, 2 * t + 2)
                    dve.bn_stats(stats[:, t, :], acc[:, t, :]).then_inc(s_st, 1)
                for t in range(4 * q, 4 * q + 4):
                    dve.wait_ge(s_st, t + 1)
                    dve.bn_aggr(mv[:, t, :], stats[:, t, :]).then_inc(s_mv, 1)
                dve.wait_ge(s_sd, q + 1)
                dve.reciprocal(rstd[:, 4 * q:4 * q + 4], sd[:, 4 * q:4 * q + 4]).then_inc(s_rstd, 1)
                dve.wait_ge(s_rstd, q + 1)
                for t in range(4 * q, 4 * q + 4):
                    ts = dve.tensor_scalar(acc[:, t, :], acc[:, t, :], mv[:, t, 0:1], rstd[:, t:t + 1],
                                           ALU.subtract, ALU.mult)
                ts.then_inc(s_fin, 1)


def build(nc, A, out):
    with ExitStack() as ctx:
        def sb(name, shape, dt=F32):
            return ctx.enter_context(nc.sbuf_tensor(name, shape, dt))

        keep = {"hln": sb("hln", [P, TILES, M]), "xT": sb("xT", [P, 2, TOKENS]),
                "small": sb("small", [P, SMALL]), "eps": sb("eps", [P, 1]),
                "raw1": sb("raw1", [P, 2, I]), "raw2": sb("raw2", [P, IC, M])}
        keep["bank"] = [ctx.enter_context(nc.psum_tensor(f"bank{i}", [P, 512], F32))[:] for i in range(8)]
        for n in ("s_raw1", "s_raw2", "s_zero"):
            keep[n] = ctx.enter_context(nc.semaphore(n))
        front(nc, A, keep)
        experts(nc, A, keep, out)


def kernel(**inputs):
    import concourse.bacc as bacc
    from concourse.bass_utils import run_bass_kernel_spmd

    nc = bacc.Bacc("TRN2", target_bir_lowering=False, num_devices=1)
    given = {k.split("_", 2)[-1] if k.startswith("L0") else k: np.asarray(v) for k, v in inputs.items()}
    fwd, inv, small = shape_constants()
    tables = {"fwd_table": fwd, "inv_table": inv, "small_table": small}
    for n in ("x", "scharr", "A_log", "D", "C_re", "log_dt", "Wr1", "br1", "Wr2", "br2"):
        tables[n] = given[n]
    for n in ("W1", "b1", "W2", "b2"):
        tables[n] = np.concatenate([given[n[0] + "e" + n[1]], given[n[0] + "s" + n[1]][None]])
    arrays, A = {}, {}
    for n, a in tables.items():
        arrays[f"in_{n}_dram"] = np.ascontiguousarray(a)
        A[n] = nc.dram_tensor(f"in_{n}_dram", a.shape, mybir.dt.from_np(a.dtype), kind="ExternalInput").ap()
    for n in ("xs_d", "ys_d"):
        A[n] = nc.dram_tensor(n, (SLOTS * T, M), F32, kind="Internal").ap()
    out = nc.dram_tensor("out_dram", (B, L, M), F32, kind="ExternalOutput").ap()
    build(nc, A, out)
    r = run_bass_kernel_spmd(nc, [arrays], core_ids=[0])
    return r.results[0]["out_dram"]
```

```python
from contextlib import ExitStack

import concourse.bass as bass
import numpy as np
from concourse import mybir

F32 = mybir.dt.float32
F32R = mybir.dt.float32r
I32 = mybir.dt.int32
U32 = mybir.dt.uint32
ALU = mybir.AluOpType
ACT = mybir.ActivationFunctionType
X = mybir.AxisListType.X

P = 128
B, COLORS, L, M = 8, 3, 256, 256
LH = L // P
TILES = B * LH
PAIRS = B // 2
W2 = 2 * M
N_STATE = 64
MP = M // 2
Q = 32
NB = L // Q
GRAY = (0.2989, 0.587, 0.114)
EPS = 1e-5

TOKENS = B * L
E, K_TOP = 8, 2
I, IC = 1024, 8
PAIRS1 = IC // 2
R1 = M // 4
T = 256
SHARED = TOKENS // T
SLOTS = K_TOP * TOKENS // T + E - 1
SLOTS += SLOTS % 2
GR = 8
SMALL = 9 * P + E * E
ZPARTS = 12
SOFT, SOFT2 = 4, 21


def shape_constants():
    pos, freq = np.arange(P)[:, None], np.arange(P)[None, :]

    def waves(n, k):
        ang = np.pi * (n * (2 * k + 1) % (4 * P)) / (2 * P)
        return [np.cos(ang), -np.sin(ang)]

    behind = [w * (pos > 0) for w in waves(pos - P, freq)]
    inverse = [w / P for w in waves(freq, pos)]
    dft = np.stack(waves(pos, freq) + behind + inverse, 1)
    row, col = pos, freq
    bands = [(row - col == dy - 1) for dy in range(3)]
    ramp = np.broadcast_to(col, (P, P))
    seam = np.zeros((P, 2, P))
    seam[0:3, 0, P - 1] = 1
    seam[3:6, 1, 0] = 1
    upto = np.broadcast_to((np.arange(E)[None, :] <= np.arange(E)[:, None]).reshape(1, -1), (P, E * E))
    small = np.concatenate([np.stack(bands + [row == col, row < col, np.ones((P, P)), ramp], 1).reshape(P, -1),
                            seam.reshape(P, -1), upto], 1)
    return np.ascontiguousarray(dft.reshape(P, -1), np.float32), np.ascontiguousarray(small, np.float32)


def front(nc, A, keep):
    hln, xT, scratch = keep["hln"], keep["xT"], keep["scratch"]
    small, eps_t, bank, wr1, br1 = keep["small"], keep["eps"], keep["bank"], keep["wr1"], keep["br1"]
    BAND = [small[:, i * P:(i + 1) * P] for i in range(3)]
    IDENT = small[:, 3 * P:4 * P]
    RAMP = small[:, 6 * P:7 * P]
    SEAM = [small[0:6, (7 + i) * P:(8 + i) * P] for i in range(2)]
    with ExitStack() as ctx:
        def sb(name, shape, dt=F32):
            return ctx.enter_context(nc.sbuf_tensor(name, shape, dt))

        def sem(name):
            return ctx.enter_context(nc.semaphore(name))

        NX = 3
        image = sb("image", [P, NX, COLORS, LH, M])
        gray = sb("gray", [P, LH, B, M + 2])
        edge_rows = sb("edge_rows", [6, B, M])
        dft = sb("dft", [P, 6, P])
        taps = sb("taps", [P, 2, 3, 3])
        seam_taps = sb("seam_taps", [6, 2])
        stencil = sb("stencil", [P, 2, 3, P])
        seam = sb("seam", [6, 2, 2, P])
        half_abs = sb("half_abs", [P, 2, 2, W2])
        h = sb("h", [P, LH, PAIRS, W2])
        log_dt = sb("log_dt", [P, MP])
        a_log = sb("a_log", [P, 1])
        a_exp = sb("a_exp", [P, 1])
        dt_exp = sb("dt_exp", [P, MP])
        neg_dta = sb("neg_dta", [P, MP])
        far = sb("far", [P, MP, NB])
        c_in = sb("c_in", [P, 2, N_STATE])
        d_row = sb("d_row", [1, M])
        zero = sb("zero", [P, SLOTS * T * M // P // ZPARTS])
        taps_k = sb("taps_k", [P, LH, M])
        kf = sb("kf", [P, 2, 3, M])
        prod = sb("prod", [P, 3, 2, 2, W2])
        spec = sb("spec", [P, 3, 2, W2])
        stats = sb("stats", [P, TILES, 6])
        mv = sb("mv", [P, TILES, 2])
        sd = sb("sd", [P, TILES])
        rstd = sb("rstd", [P, TILES])
        decay = hln[:].rearrange("p t m -> p (t m)").rearrange("p (m q) -> p m q", q=Q)
        c_decay = scratch[:].rearrange("p (m h b) -> p m h b", h=2, b=NB)
        kq = xT[0:Q, 0, :].rearrange("q (b m) -> q b m", b=NB)
        r1T = scratch[0:R1, :]

        s_image = [sem(f"s_image{i}") for i in range(NX)]
        s_const, s_dt, s_taps, s_dft, s_c = sem("s_const"), sem("s_dt"), sem("s_taps"), sem("s_dft"), sem("s_c")
        s_pad = sem("s_pad")
        s_gray1 = sem("s_gray1")
        s_gray2 = sem("s_gray2")
        s_gray = sem("s_gray")
        s_rows = [sem(f"s_rows{i}") for i in range(PAIRS)]
        s_st0, s_stencil = sem("s_st0"), sem("s_stencil")
        s_edge = sem("s_edge")
        s_abs, s_h = sem("s_abs"), sem("s_h")
        s_exp0, s_dta, s_farg, s_far = sem("s_exp0"), sem("s_dta"), sem("s_farg"), sem("s_far")
        s_ct, s_cz, s_cd = sem("s_ct"), sem("s_cz"), sem("s_cd")
        s_arg, s_decay, s_ksum = sem("s_arg"), sem("s_decay"), sem("s_ksum")
        s_kq, s_relay, s_kd, s_kf, s_kfc = sem("s_kq"), sem("s_relay"), sem("s_kd"), sem("s_kf"), sem("s_kfc")
        s_u = sem("s_u")
        s_prod, s_diff, s_spec = sem("s_prod"), sem("s_diff"), sem("s_spec")
        s_y = sem("s_y")
        s_stat, s_mv, s_sd, s_rstd = sem("s_stat"), sem("s_mv"), sem("s_sd"), sem("s_rstd")
        s_ln = sem("s_ln")
        s_xt, s_xtc = sem("s_xt"), sem("s_xtc")
        s_r1 = sem("s_r1")
        s_early = keep["s_early"]

        EDGE = [bank[0], bank[1]]
        YB = [bank[2], bank[3]]
        KFB = YB
        SPECTRA = keep["psum"][:, 4:8, :]
        KSUM = [bank[4 + i] for i in range(4)]
        block = ctx.enter_context(nc.Block())

        @block.sync
        def _(sp):
            x = A["x"]

            def load_image(b):
                if b >= NX:
                    sp.wait_ge(s_gray, b - NX + 1)
                sp.dma_start(image[:, b % NX], x[b].rearrange("c (q p) m -> p (c q) m", p=P)
                             ).then_inc(s_image[b % NX], 16)

            def seam_rows(g):
                sp.wait_ge(s_pad, 2)
                sp.wait_ge(s_gray, 2 * g + 2)
                for k, (p, lh) in enumerate(((0, 1), (P - 1, 0))):
                    for dx in range(3):
                        sp.dma_start(edge_rows[3 * k + dx:3 * k + dx + 1, 2 * g:2 * g + 2, :],
                                     gray[p:p + 1, lh, 2 * g:2 * g + 2, dx:dx + M]).then_inc(s_rows[g], 16)

            for b in range(NX):
                load_image(b)
            sp.dma_start(dft[:].rearrange("p a b -> p (a b)"), A["dft_table"]).then_inc(s_dft, 16)
            seam_rows(0)
            load_image(3)
            load_image(4)
            seam_rows(1)
            load_image(5)
            sp.dma_start(keep["raw1"][:], A["W1"][E].rearrange("(c p) i -> p c i", p=P)).then_inc(keep["s_raw1"], 16)
            sp.dma_start(keep["raw2"][:], A["W2"][E].rearrange("(a p) c -> p a c", p=P)).then_inc(keep["s_raw2"], 16)
            load_image(6)
            seam_rows(2)
            load_image(7)
            seam_rows(3)
            n = zero.shape[1]
            sp.wait_ge(s_pad, 4)
            for i in range(ZPARTS):
                sp.dma_start(A["xs_d"].rearrange("(p r) c -> p (r c)", p=P)[:, i * n:(i + 1) * n], zero[:]
                             ).then_inc(keep["s_zero"], 16)
            sp.wait_ge(keep["s_zero"], ZPARTS * 16)

        @block.gpsimd
        def _(pool):
            pool.memset(gray[:, :, :, 0:1], 0.0).then_inc(s_pad, 1)
            pool.memset(gray[:, :, :, M + 1:M + 2], 0.0).then_inc(s_pad, 1)
            pool.memset(c_decay, 0.0).then_inc(s_cz, 1)
            pool.memset(eps_t[:], EPS).then_inc(s_pad, 1)
            pool.memset(zero[:], 0.0).then_inc(s_pad, 1)

            def sum_filters(n):
                g, lh = n // 2, n % 2
                pool.wait_ge(s_abs, 2 * n + 2)
                pool.tensor_tensor(h[:, lh, g, :], half_abs[:, lh, 0, :], half_abs[:, lh, 1, :],
                                   ALU.add).then_inc(s_h, 1)

            def sum_products(g):
                for k in range(3):
                    pool.wait_ge(s_prod, 6 * g + 2 * k + 2)
                    if g and k == 0:
                        pool.wait_ge(s_y, LH * g)
                    pool.tensor_tensor(spec[:, k, 0, :], prod[:, k, 0, 0, :], prod[:, k, 0, 1, :],
                                       ALU.subtract).then_inc(s_diff, 1)
                    pool.tensor_tensor(spec[:, k, 1, :], prod[:, k, 1, 0, :], prod[:, k, 1, 1, :],
                                       ALU.add).then_inc(s_diff, 1)
                pool.wait_ge(s_diff, 6 * g + 6)
                pool.tensor_tensor(spec[:, 2], spec[:, 1], spec[:, 2], ALU.add).then_inc(s_spec, 1)

            sum_filters(0)
            sum_filters(1)
            sum_filters(2)
            sum_filters(3)
            for g in range(PAIRS):
                sum_products(g)
                if g + 2 < PAIRS:
                    sum_filters(2 * g + 4)
                    sum_filters(2 * g + 5)

        @block.scalar
        def _(act):
            act.dma_start(taps[:].rearrange("p f y x -> p (f y x)"),
                          A["scharr"].rearrange("f a y x -> (f a y x)").partition_broadcast(P)).then_inc(s_taps, 16)
            for k, dy in enumerate((2, 0)):
                for f in range(2):
                    act.dma_start(seam_taps[3 * k:3 * k + 3, f:f + 1],
                                  A["scharr"][f, 0, dy, :].rearrange("(n a) -> n a", a=1)).then_inc(s_taps, 16)
            act.dma_start(small[:], A["small_table"]).then_inc(s_const, 16)
            for half in range(2):
                act.dma_start(log_dt[64 * half:64 * half + 64, :],
                              A["log_dt"][half * MP:(half + 1) * MP].partition_broadcast(64)).then_inc(s_dt, 16)
                act.dma_start(a_log[64 * half:64 * half + 64, :],
                              A["A_log"].rearrange("(n a) -> n a", a=1)).then_inc(s_dt, 16)
            act.dma_start(c_in[:], A["C_re"].rearrange("(a p) n -> p a n", p=P)).then_inc(s_c, 16)
            act.dma_start(d_row[:], A["D"].rearrange("(a m) -> a m", a=1)).then_inc(s_c, 16)

            act.wait_ge(s_dt, 64)
            act.activation(a_exp[:], a_log[:], ACT.Exp).then_inc(s_exp0, 1)
            act.activation(dt_exp[:], log_dt[:], ACT.Exp).then_inc(s_exp0, 1)

            def gray_first(b):
                act.wait_ge(s_image[b % NX], 16 * (b // NX + 1))
                act.activation(gray[:, :, b, 1:M + 1], image[:, b % NX, 0], ACT.Copy,
                               scale=GRAY[0]).then_inc(s_gray1, 1)

            def abs_edges(n):
                for f in range(2):
                    act.wait_ge(s_edge, 2 * n + f + 1)
                    if n >= 2:
                        act.wait_ge(s_h, n - 1)
                    act.activation(half_abs[:, n % 2, f, :], EDGE[f], ACT.Abs, scale=0.5).then_inc(s_abs, 1)

            def deviation(g):
                act.wait_ge(s_mv, 4 * g + 4)
                act.activation(sd[:, 4 * g:4 * g + 4], mv[:, 4 * g:4 * g + 4, 1], ACT.Sqrt,
                               bias=eps_t[:, 0:1]).then_inc(s_sd, 1)

            def copy_xt(g):
                for c in range(2):
                    act.wait_ge(s_xt, 2 * g + c + 1)
                    act.activation(xT[:, c, g * W2:(g + 1) * W2], YB[c], ACT.Copy).then_inc(s_xtc, 1)

            def relu(g):
                act.wait_ge(s_r1, g + 1)
                act.activation(r1T[:, g * W2:(g + 1) * W2], EDGE[g % 2][0:R1, :], ACT.Relu,
                               bias=br1[:, 0:1]).then_inc(keep["s_relu"], 1)

            gray_first(0)
            gray_first(1)
            act.wait_ge(s_farg, 1)
            act.activation(far[:], far[:], ACT.Exp, scale=float(Q)).then_inc(s_far, 1)
            for c in range(2):
                act.wait_ge(s_arg, c + 1)
                part = decay[:, c * MP // 2:(c + 1) * MP // 2, :]
                act.activation(part, part, ACT.Exp).then_inc(s_decay, 1)
            act.dma_start(wr1[:], A["Wr1"].rearrange("(c p) r -> p c r", p=P)).then_inc(s_early, 16)
            act.dma_start(br1[:], A["br1"].rearrange("(r a) -> r a", a=1)).then_inc(s_early, 16)
            act.dma_start(keep["wr2"][:], A["Wr2"]).then_inc(s_early, 16)
            act.dma_start(keep["br2"][:], A["br2"].partition_broadcast(P)).then_inc(s_early, 16)
            act.dma_start(keep["b1_in"][:], A["b1"].rearrange("e (a p) -> (e a) p", p=P)).then_inc(s_early, 16)
            act.dma_start(keep["b2_rows"][:].rearrange("p e m -> p (e m)"),
                          A["b2"].rearrange("e m -> (e m)").partition_broadcast(P)).then_inc(s_early, 16)
            gray_first(2)
            abs_edges(0)
            abs_edges(1)
            gray_first(3)
            for i in range(4):
                act.wait_ge(s_ksum, i + 1)
                n = MP // 4
                act.activation(kq.rearrange("q b (h m) -> q m h b", h=2)[:, i * n:(i + 1) * n],
                               KSUM[i][0:Q, :].rearrange("q (m h b) -> q m h b", h=2, b=NB), ACT.Copy).then_inc(s_kq, 1)
            act.wait_ge(s_kq, 4)
            for i in range(P // Q):
                act.dma_start(taps_k[Q * i:Q * i + Q, :, :], kq[:, i::P // Q, :]).then_inc(s_relay, 16)
            gray_first(4)
            abs_edges(2)
            gray_first(5)
            abs_edges(3)
            for k in range(2):
                act.wait_ge(s_kf, k + 1)
                act.activation(kf[:, k, 0:2, :].rearrange("p a m -> p (a m)"), KFB[k], ACT.Copy).then_inc(s_kfc, 1)
                act.activation(kf[:, k, 2, :], KFB[k][:, 0:M], ACT.Copy).then_inc(s_kfc, 1)
            gray_first(6)
            abs_edges(4)
            gray_first(7)
            abs_edges(5)
            act.wait_ge(s_pad, 3)
            deviation(0)
            abs_edges(6)
            copy_xt(0)
            abs_edges(7)
            act.wait_ge(s_early, 96)
            deviation(1)
            copy_xt(1)
            relu(0)
            deviation(2)
            copy_xt(2)
            relu(1)
            relu(2)
            deviation(3)
            copy_xt(3)
            relu(3)

        @block.tensor
        def _(pe):
            def edges(n):
                g, lh = n // 2, n % 2
                if lh == 0:
                    pe.wait_ge(s_gray, 2 * g + 2)
                for f in range(2):
                    if n:
                        pe.wait_ge(s_abs, 2 * n - 1 + f)
                    for dx in range(3):
                        pe.matmul(EDGE[f], stencil[:, f, dx, :], gray[:, lh, 2 * g:2 * g + 2, dx:dx + M],
                                  start=(dx == 0), stop=False)
                pe.wait_ge(s_rows[g], 16 * 6)
                for f in range(2):
                    pe.matmul(EDGE[f], seam[:, f, lh, :], edge_rows[:, 2 * g:2 * g + 2, :],
                              start=False, stop=True).then_inc(s_edge, 1)

            def spectra(g):
                for j in range(2):
                    pe.wait_ge(s_h, 2 * g + j + 1)
                    if g:
                        pe.wait_ge(s_prod, 6 * (g - 1) + (4 if j == 0 else 6))
                    for ri in range(2):
                        mm = pe.matmul(SPECTRA[:, 2 * j + ri, :], dft[:, ri, :], h[:, j, g, :], start=True, stop=True)
                    mm.then_inc(s_u, 1)

            def convolved(g):
                if g:
                    pe.wait_ge(s_xtc, 2 * g)
                else:
                    pe.wait_ge(s_kfc, 4)
                for lh in range(LH):
                    if lh == 0:
                        pe.wait_ge(s_diff, 6 * g + 2)
                    else:
                        pe.wait_ge(s_spec, g + 1)
                    for ri in range(2):
                        mm = pe.matmul(YB[lh], dft[:, 4 + ri, :], spec[:, 2 * lh, ri, :], start=(ri == 0), stop=(ri == 1))
                    mm.then_inc(s_y, 1)

            def transposes(g):
                pe.wait_ge(s_ln, g + 1)
                for c in range(2):
                    for t in range(4):
                        mm = pe.transpose(YB[c][:, t * P:(t + 1) * P], hln[:, 4 * g + t, c * P:(c + 1) * P], IDENT)
                    mm.then_inc(s_xt, 1)

            def hidden(g):
                if g == 0:
                    pe.wait_ge(s_early, 96)
                    pe.wait_ge(s_abs, 4 * PAIRS)
                if g >= 2:
                    pe.wait_ge(keep["s_relu"], g - 1)
                pe.wait_ge(s_xtc, 2 * g + 2)
                for c in range(2):
                    mm = pe.matmul(EDGE[g % 2][0:R1, :], wr1[:, c, :], xT[:, c, g * W2:(g + 1) * W2],
                                   start=(c == 0), stop=(c == 1))
                mm.then_inc(s_r1, 1)

            pe.wait_ge(s_const, 16)
            pe.wait_ge(s_c, 32)
            pe.transpose(bank[2][:, 0:P], c_in[:].rearrange("p a n -> p (a n)"), IDENT).then_inc(s_ct, 1)
            pe.wait_ge(s_stencil, 6 + 4)
            pe.wait_ge(s_pad, 2)
            edges(0)
            edges(1)
            pe.wait_ge(s_cd, 2)
            for mp in range(MP):
                if mp % (MP // 2) == 0:
                    pe.wait_ge(s_decay, mp // (MP // 2) + 1)
                i, n = mp // (MP // 4), mp % (MP // 4)
                mm = pe.matmul(KSUM[i][0:Q, 2 * NB * n:2 * NB * (n + 1)], decay[:, mp, :],
                               c_decay[:, mp].rearrange("p h b -> p (h b)"), start=True, stop=True)
                if n == MP // 4 - 1:
                    mm.then_inc(s_ksum, 1)
            edges(2)
            edges(3)
            pe.wait_ge(s_kd, 1)
            pe.wait_ge(s_dft, 16)
            for ri in range(2):
                mm = pe.matmul(KFB[0][:, ri * M:(ri + 1) * M], dft[:, ri, :], taps_k[:, 0, :], start=True, stop=True)
            mm.then_inc(s_kf, 1)
            for ri in range(2):
                pe.matmul(KFB[1][:, ri * M:(ri + 1) * M], dft[:, 2 + ri, :], taps_k[:, 0, :], start=True, stop=False)
                mm = pe.matmul(KFB[1][:, ri * M:(ri + 1) * M], dft[:, ri, :], taps_k[:, 1, :], start=False, stop=True)
            mm.then_inc(s_kf, 1)
            spectra(0)
            edges(4)
            edges(5)
            convolved(0)
            spectra(1)
            edges(6)
            transposes(0)
            edges(7)
            convolved(1)
            spectra(2)
            transposes(1)
            hidden(0)
            convolved(2)
            spectra(3)
            transposes(2)
            hidden(1)
            hidden(2)
            convolved(3)
            transposes(3)
            hidden(3)

        @block.vector
        def _(dve):
            dve.wait_ge(s_exp0, 2)
            dve.tensor_scalar(neg_dta[:], dt_exp[:], a_exp[:, 0:1], -1.0, ALU.mult, ALU.mult).then_inc(s_dta, 1)
            dve.wait_ge(s_const, 16)
            dve.wait_ge(s_dta, 1)
            dve.tensor_tensor(far[:], neg_dta[:].unsqueeze(2).broadcast_to([P, MP, NB]),
                              RAMP[:, 0:NB].unsqueeze(1).broadcast_to([P, MP, NB]), ALU.mult).then_inc(s_farg, 1)
            for c in range(2):
                part = slice(c * MP // 2, (c + 1) * MP // 2)
                dve.tensor_tensor(decay[:, part, :], neg_dta[:, part].unsqueeze(2).broadcast_to([P, MP // 2, Q]),
                                  RAMP[:, 0:Q].unsqueeze(1).broadcast_to([P, MP // 2, Q]), ALU.mult).then_inc(s_arg, 1)
            dve.wait_ge(s_taps, 80)
            for dy in range(3):
                if dy:
                    dve.wait_ge(s_st0, 6 * dy)
                for f in range(2):
                    for dx in range(3):
                        tap = taps[:, f, dy, dx:dx + 1]
                        if dy == 0:
                            st = dve.tensor_scalar(stencil[:, f, dx, :], BAND[0], tap, None, ALU.mult)
                        else:
                            st = dve.scalar_tensor_tensor(stencil[:, f, dx, :], BAND[dy], tap,
                                                          stencil[:, f, dx, :], ALU.mult, ALU.add)
                        st.then_inc(s_st0 if dy < 2 else s_stencil, 1)
            for f in range(2):
                for lh in range(LH):
                    dve.tensor_scalar(seam[:, f, lh, :], SEAM[lh], seam_taps[:, f:f + 1], None,
                                      ALU.mult).then_inc(s_stencil, 1)

            def gray_rest(b):
                dve.wait_ge(s_gray1, b + 1)
                for c in (1, 2):
                    if c == 2:
                        dve.wait_ge(s_gray2, b + 1)
                    dve.scalar_tensor_tensor(gray[:, :, b, 1:M + 1], image[:, b % NX, c], GRAY[c],
                                             gray[:, :, b, 1:M + 1], ALU.mult, ALU.add
                                             ).then_inc(s_gray2 if c == 1 else s_gray, 1)

            gray_rest(0)
            gray_rest(1)
            dve.wait_ge(s_ct, 1)
            dve.wait_ge(s_cz, 1)
            dve.wait_ge(s_far, 1)
            for mh in range(2):
                r = slice(64 * mh, 64 * mh + 64)
                dve.tensor_tensor(c_decay[r, :, mh, :], bank[2][r, 0:P].unsqueeze(2).broadcast_to([64, MP, NB]),
                                  far[r], ALU.mult).then_inc(s_cd, 1)
            for b in range(2, 6):
                gray_rest(b)
            dve.wait_ge(s_relay, 16 * P // Q)
            dve.scalar_tensor_tensor(taps_k[0:1, 0], d_row[:], 1.0, taps_k[0:1, 0], ALU.add, ALU.add
                                     ).then_inc(s_kd, 1)

            def products(g):
                for n, (k, j) in enumerate(((0, 0), (1, 0), (0, 1))):
                    dve.wait_ge(s_u, 2 * g + j + 1)
                    if g:
                        dve.wait_ge(s_diff, 6 * (g - 1) + 2 * n + 2)
                    for kind in range(2):
                        dve.tensor_tensor(prod[:, n, kind].rearrange("p r (b m) -> p r b m", b=2),
                                          SPECTRA[:, 2 * j:2 * j + 2, :].rearrange("p r (b m) -> p r b m", b=2),
                                          kf[:, k, kind:kind + 2, :].unsqueeze(2).broadcast_to([P, 2, 2, M]),
                                          ALU.mult).then_inc(s_prod, 1)

            def layernorm(g):
                for lh in range(LH):
                    dve.wait_ge(s_y, LH * g + lh + 1)
                    for b in range(2):
                        t = 4 * g + 2 * b + lh
                        dve.bn_stats(stats[:, t, :], YB[lh][:, b * M:(b + 1) * M]).then_inc(s_stat, 1)
                dve.wait_ge(s_stat, 4 * g + 4)
                for t in range(4 * g, 4 * g + 4):
                    dve.bn_aggr(mv[:, t, :], stats[:, t, :]).then_inc(s_mv, 1)
                dve.wait_ge(s_sd, g + 1)
                dve.reciprocal(rstd[:, 4 * g:4 * g + 4], sd[:, 4 * g:4 * g + 4]).then_inc(s_rstd, 1)
                dve.wait_ge(s_rstd, g + 1)
                for lh in range(LH):
                    for b in range(2):
                        t = 4 * g + 2 * b + lh
                        ts = dve.tensor_scalar(hln[:, t, :], YB[lh][:, b * M:(b + 1) * M], mv[:, t, 0:1],
                                               rstd[:, t:t + 1], ALU.subtract, ALU.mult)
                ts.then_inc(s_ln, 1)

            dve.wait_ge(s_kfc, 4)
            products(0)
            gray_rest(6)
            gray_rest(7)
            for g in range(1, PAIRS):
                layernorm(g - 1)
                products(g)
            layernorm(PAIRS - 1)


def experts(nc, A, keep, out):
    hln, xT, small, eps_t, bank = (keep[k] for k in ("hln", "xT", "small", "eps", "bank"))
    raw1, raw2, s_raw1, s_raw2 = (keep[k] for k in ("raw1", "raw2", "s_raw1", "s_raw2"))
    wr2, br2, b1_in, b2_rows = (keep[k] for k in ("wr2", "br2", "b1_in", "b2_rows"))
    r1T = keep["scratch"][0:R1, :]
    BEFORE, ONES, RAMP = small[:, 4 * P:5 * P], small[:, 5 * P:6 * P], small[:, 6 * P:7 * P]
    IDENT = small[:, 3 * P:4 * P]
    UPTO = small[:, 9 * P:9 * P + E * E].rearrange("p (e f) -> p e f", f=E)
    with ExitStack() as ctx:
        def sb(name, shape, dt=F32):
            return ctx.enter_context(nc.sbuf_tensor(name, shape, dt))

        def sem(name):
            return ctx.enter_context(nc.semaphore(name))

        b1T = sb("b1T", [P, (E + 1) * IC])
        b1_now = sb("b1_now", [P, 2, IC])
        w1_hi, w1_lo = sb("w1_hi", [P, 2, 2, I], F32R), sb("w1_lo", [P, 2, 2, I], F32R)
        w2_hi, w2_lo = sb("w2_hi", [P, 2, IC, M], F32R), sb("w2_lo", [P, 2, IC, M], F32R)
        x_hi, x_lo = sb("x_hi", [P, 2, 2, T], F32R), sb("x_lo", [P, 2, 2, T], F32R)
        h1 = keep["scratch"][:].rearrange("p (a t) -> p a t", t=T)
        rows = keep["scratch"][:].rearrange("p (n m) -> p n m", m=M)
        h1_hi, h1_lo = sb("h1_hi", [P, 2, IC, T], F32R), sb("h1_lo", [P, 2, IC, T], F32R)
        xs = sb("xs", [P, 2, 2, M])
        acc = sb("acc", [P, TILES, M])
        y = sb("y", [P, 2, 2, M])

        def rt(name, shape=(P, TILES, E), dt=F32):
            return sb(name, list(shape), dt)
        logit, eq, key, rank = rt("logit"), rt("eq"), rt("key"), rt("rank")
        pick = [rt("pick0"), rt("pick1")]
        best = [rt("best0", (P, TILES)), rt("best1", (P, TILES))]
        both = rt("both")
        col, col2 = rt("col", (P, TILES)), rt("col2", (P, TILES))
        gate_w = rt("gate_w", (P, 2, TILES))
        rev = rt("rev", (P, E))
        n_exp, slots_e, end_e, base_e = (rt(n, (P, E)) for n in ("n_exp", "slots_e", "end_e", "base_e"))
        cmp = rt("cmp", (P, max(SLOTS, E), E))
        pos = rt("pos", (P, 2, TILES), I32)
        slot_f = rt("slot_f", (P, SLOTS))
        slot_e = rt("slot_e", (P, SLOTS), I32)
        stats, mv = sb("stats2", [P, TILES, 6]), sb("mv2", [P, TILES, 2])
        sd, rstd = sb("sd2", [P, TILES]), sb("rstd2", [P, TILES])

        s_logit = sem("s_logit")
        s_b1t, s_b1c = sem("s_b1t"), sem("s_b1c")
        s_soft = sem("s_soft")
        s_ro = sem("s_ro")
        s_picked = sem("s_picked")
        s_rank = sem("s_rank")
        s_pos = sem("s_pos")
        s_acc0 = sem("s_acc0")
        s_scat = sem("s_scat")
        s_w1h, s_w1l, s_w2h, s_w2l = sem("s_w1h"), sem("s_w1l"), sem("s_w2h"), sem("s_w2l")
        s_xs = [sem("s_xs0"), sem("s_xs1")]
        s_xt, s_xh, s_xl = sem("s_xt2"), sem("s_xh"), sem("s_xl")
        s_bias = sem("s_bias")
        s_g1, s_silu, s_hhi, s_hlo, s_g2 = sem("s_g1"), sem("s_silu"), sem("s_hhi"), sem("s_hlo"), sem("s_g2")
        s_y = sem("s_y2")
        s_store = [sem("s_store0"), sem("s_store1")]
        s_rows = [sem(f"s_rows2_{i}") for i in range(GR)]
        s_mix, s_used = sem("s_mix"), sem("s_used")
        s_st, s_mv, s_sd, s_rstd, s_fin = sem("s_st2"), sem("s_mv2"), sem("s_sd2"), sem("s_rstd2"), sem("s_fin")
        s_out = sem("s_out")

        G2 = [bank[4], bank[5]]
        XB, RB = bank[6], bank[7]
        xs_d, ys_d = A["xs_d"], A["ys_d"]
        block = ctx.enter_context(nc.Block())

        @block.sync
        def _(sp):
            def load_w1(v, e):
                sp.wait_ge(s_w1l, v)
                sp.dma_start(raw1[:], A["W1"][e].rearrange("(c p) i -> p c i", p=P)).then_inc(s_raw1, 16)

            def load_w2(v, e):
                sp.wait_ge(s_w2l, v)
                sp.dma_start(raw2[:], A["W2"][e].rearrange("(a p) c -> p a c", p=P)).then_inc(s_raw2, 16)

            def load_x(s, par, first=False):
                if not first:
                    sp.wait_ge(s_xt, s - 1)
                sp.dma_start(xs[:, par], xs_d[bass.ds(s * T, T), :].rearrange("(j p) c -> p j c", p=P)
                             ).then_inc(s_xs[par], 16)

            def store_y(s, par):
                sp.wait_ge(s_y, SHARED + s + 1)
                sp.dma_start(ys_d[bass.ds(s * T, T), :].rearrange("(j p) c -> p j c", p=P), y[:, par]
                             ).then_inc(s_store[par], 16)

            def expert_of(s):
                return sp.value_load(slot_e[0:1, bass.ds(s, 1)], min_val=0, max_val=E - 1)

            def slot(s, par, static=True):
                if not static or s + 1 < SLOTS:
                    load_w1(s + 2, expert_of(s + 1))
                    load_x(s + 1, 1 - par, first=static and s == 0)
                load_w2(s + 1, expert_of(s))
                if not static or s >= 2:
                    store_y(s - 2, par)

            sp.wait_ge(s_pos, 1)
            load_w1(1, expert_of(0))
            sp.wait_ge(s_scat, 16 * 2 * TILES)
            load_x(0, 0, first=True)
            slot(0, 0)
            slot(1, 1)
            with sp.Fori(2, SLOTS - 3, 2) as s:
                slot(s, 0, static=False)
                slot(s + 1, 1, static=False)
            for s in range(SLOTS - 2, SLOTS):
                slot(s, s % 2)
            store_y(SLOTS - 2, 0)
            store_y(SLOTS - 1, 1)
            for q in range(4):
                sp.wait_ge(s_fin, q + 1)
                sp.dma_start(out[2 * q:2 * q + 2].rearrange("b (h p) m -> p (b h) m", p=P),
                             acc[:, 4 * q:4 * q + 4, :]).then_inc(s_out, 16)
            sp.wait_ge(s_out, 64)

        @block.gpsimd
        def _(pool):
            for t in range(0, TILES, 4):
                pool.tensor_tensor(acc[:, t:t + 4, :], hln[:, t:t + 4, :],
                                   b2_rows[:, E:E + 1, :].broadcast_to([P, 4, M]), ALU.add).then_inc(s_acc0, 1)
            pool.wait_ge(s_pos, 1)
            for t in range(TILES):
                for k in range(2):
                    pool.indirect_dma_start(xs_d, bass.IndirectOffsetOnAxis(ap=pos[:, k, t:t + 1].bitcast(U32), axis=0),
                                            hln[:, t, :], None).then_inc(s_scat, 16)

            def lo(u, par):
                for j in range(PAIRS1):
                    pool.wait_ge(s_hhi, PAIRS1 * u + j + 1)
                    pool.tensor_tensor(h1_lo[:, par, 2 * j:2 * j + 2, :], h1[:, 2 * j:2 * j + 2, :],
                                       h1_hi[:, par, 2 * j:2 * j + 2, :].bitcast(F32), ALU.subtract).then_inc(s_hlo, 1)

            with pool.Fori(SHARED, SHARED + SLOTS - 1, 2) as u:
                lo(u, 0)
                lo(u + 1, 1)
            for par in range(2):
                pool.wait_ge(s_store[par], 16 * (SLOTS // 2))
            for n in range(2 * TILES):
                if n >= GR:
                    pool.wait_ge(s_mix, n - GR + 1)
                pool.indirect_dma_start(rows[:, n % GR, :], None, ys_d,
                                        bass.IndirectOffsetOnAxis(ap=pos[:, n % 2, n // 2:n // 2 + 1].bitcast(U32), axis=0)
                                        ).then_inc(s_rows[n % GR], 16)

        @block.scalar
        def _(act):
            def w1h(v, par, first=False):
                act.wait_ge(s_raw1, 16 * v + 16)
                if not first:
                    act.wait_ge(s_g1, PAIRS1 * (v + SHARED - 2))
                act.activation(w1_hi[:, par], raw1[:], ACT.Copy).then_inc(s_w1h, 1)

            def w2h(v, par, first=False):
                act.wait_ge(s_raw2, 16 * v + 16)
                if not first:
                    act.wait_ge(s_g2, v + SHARED - 2)
                act.activation(w2_hi[:, par], raw2[:], ACT.Copy).then_inc(s_w2h, 1)

            def xh(u, par, shared, first=False):
                if not first:
                    act.wait_ge(s_g1, PAIRS1 * (u - 1))
                if shared:
                    src = xT[:, :, bass.ds(u * T, T)]
                else:
                    act.wait_ge(s_xt, u - SHARED + 1)
                    src = XB.rearrange("p (c t) -> p c t", c=2)
                act.activation(x_hi[:, par], src, ACT.Copy).then_inc(s_xh, 1)

            def silu(u, par, pairs, bias, shared, first=False):
                for j in pairs:
                    act.wait_ge(s_g1, PAIRS1 * u + j + 1)
                    if not first:
                        act.wait_ge(s_hlo, PAIRS1 * (u - 1) + j + 1)
                    for a in range(2):
                        ic = 2 * j + a
                        ins = act.activation(h1[:, ic, :], bank[j][:, a * T:(a + 1) * T], ACT.Silu,
                                             bias=bias[:, ic:ic + 1])
                    ins.then_inc(s_silu, 1)
                    if shared:
                        act.wait_ge(s_silu, PAIRS1 * u + j + 1)
                        act.activation(h1_hi[:, par, 2 * j:2 * j + 2, :], h1[:, 2 * j:2 * j + 2, :], ACT.Copy
                                       ).then_inc(s_hhi, 1)

            def shared_unit(u, par, first=False):
                b = b1T[:, E * IC:(E + 1) * IC]
                if not first:
                    act.wait_ge(s_g2, u - 1)
                silu(u, par, range(PAIRS1), b, True, first)

            def slot(u, par, last=False):
                s = u - SHARED
                e = act.value_load(slot_e[0:1, bass.ds(s, 1)], min_val=0, max_val=E - 1)
                act.activation(b1_now[:, par, :], b1T[:, bass.ds(e * IC, IC)], ACT.Copy).then_inc(s_bias, 1)
                act.wait_ge(s_bias, s + 1)
                silu(u, par, (0, 1), b1_now[:, par, :], False)
                if not last:
                    w1h(s + 2, par)
                silu(u, par, (2, 3), b1_now[:, par, :], False)
                if not last:
                    xh(u + 1, 1 - par, False)
                w2h(s + 1, 1 - par)

            w1h(0, 0, first=True)
            xh(0, 0, True, first=True)
            xh(1, 1, True, first=True)
            act.wait_ge(s_b1t, 1)
            act.activation(b1T[:], XB[:, 0:(E + 1) * IC], ACT.Copy).then_inc(s_b1c, 1)
            w2h(0, 0, first=True)
            act.wait_ge(s_ro, SOFT)
            act.activation(logit[:], logit[:], ACT.Exp).then_inc(s_soft, 1)
            act.wait_ge(s_ro, SOFT2)
            act.activation(col2[:], col2[:], ACT.Exp, scale=0.5).then_inc(s_soft, 1)
            act.wait_ge(s_pos, 1)
            act.wait_ge(s_b1c, 1)
            shared_unit(0, 0, first=True)
            with act.Fori(1, SHARED - 2, 2) as u:
                shared_unit(u, 1)
                xh(u + 1, 0, True)
                shared_unit(u + 1, 0)
                xh(u + 2, 1, True)
            shared_unit(SHARED - 1, 1)
            w1h(1, 1, first=True)
            xh(SHARED, 0, False)
            with act.Fori(SHARED, SHARED + SLOTS - 3, 2) as u:
                slot(u, 0)
                slot(u + 1, 1)
            slot(SHARED + SLOTS - 2, 0)
            slot(SHARED + SLOTS - 1, 1, last=True)
            for q in range(4):
                act.wait_ge(s_mv, 4 * q + 4)
                act.activation(sd[:, 4 * q:4 * q + 4], mv[:, 4 * q:4 * q + 4, 1], ACT.Sqrt,
                               bias=eps_t[:, 0:1]).then_inc(s_sd, 1)

        @block.tensor
        def _(pe):
            def g1(u, par, wpar, version, first=False):
                pe.wait_ge(s_w1l, version + 1)
                pe.wait_ge(s_xl, u + 1)
                for j in range(PAIRS1):
                    if not first:
                        pe.wait_ge(s_silu, PAIRS1 * (u - 1) + j + 1)
                    for a in range(2):
                        i0 = (2 * j + a) * P
                        parts = [(w, x) for w, x in ((w1_hi, x_hi), (w1_hi, x_lo), (w1_lo, x_hi))]
                        for n, (w, x) in enumerate(parts):
                            for c in range(2):
                                mm = pe.matmul(bank[j][:, a * T:(a + 1) * T], w[:, wpar, c, i0:i0 + P],
                                               x[:, par, c, :], start=(n == 0 and c == 0), stop=(n == 2 and c == 1))
                    mm.then_inc(s_g1, 1)

            def g2(u, par, wpar, version, first=False):
                pe.wait_ge(s_w2l, version + 1)
                if not first:
                    pe.wait_ge(s_y, u - 1)
                pe.wait_ge(s_hlo, PAIRS1 * u + PAIRS1)
                for j in range(2):
                    for ic in range(IC):
                        for n, (h, w) in enumerate(((h1_hi, w2_hi), (h1_hi, w2_lo), (h1_lo, w2_hi))):
                            mm = pe.matmul(G2[par][:, j * M:(j + 1) * M], h[:, par, ic, j * P:(j + 1) * P],
                                           w[:, wpar, ic, :], start=(ic == 0 and n == 0), stop=(ic == IC - 1 and n == 2))
                mm.then_inc(s_g2, 1)

            def transposes(s, par, count, first=False):
                pe.wait_ge(s_xs[par], count)
                if not first:
                    pe.wait_ge(s_xl, SHARED + s)
                for c in range(2):
                    for j in range(2):
                        mm = pe.transpose(XB[:, c * T + j * P:c * T + (j + 1) * P],
                                          xs[:, par, j, c * P:(c + 1) * P], IDENT)
                mm.then_inc(s_xt, 1)

            def slot(s, par, static=True):
                g1(SHARED + s, par, 1 - par, s + 1)
                if not static or s + 1 < SLOTS:
                    transposes(s + 1, 1 - par, 8 * s + (16 if par == 0 else 24))
                if static and s == 0:
                    g2(SHARED - 1, 1, 0, 0)
                else:
                    g2(SHARED + s - 1, 1 - par, par, s)

            pe.transpose(XB[:, 0:(E + 1) * IC], b1_in[:], IDENT[0:(E + 1) * IC, 0:(E + 1) * IC]).then_inc(s_b1t, 1)
            pe.wait_ge(keep["s_relu"], PAIRS)
            for t in range(TILES):
                mm = pe.matmul(RB[:, t * E:(t + 1) * E], r1T[:, t * P:(t + 1) * P], wr2[:], start=True, stop=True)
            mm.then_inc(s_logit, 1)
            g1(0, 0, 0, 0, first=True)
            pe.wait_ge(s_picked, 1)
            pe.matmul(RB[:, 128:256], BEFORE, both[:].rearrange("p t e -> p (t e)"), start=True, stop=False)
            for t in range(TILES - 1):
                n = TILES - 1 - t
                pe.matmul(RB[:, 128 + (t + 1) * E:256], ONES, both[:, t:t + 1, :].broadcast_to([P, n, E]),
                          start=False, stop=(t == TILES - 2))
            pe.matmul(RB[:, 256:256 + E], ONES, n_exp[:], start=True, stop=True).then_inc(s_rank, 1)
            g1(1, 1, 0, 0)
            g2(0, 0, 0, 0, first=True)
            g1(2, 0, 0, 0)
            g2(1, 1, 0, 0, first=True)
            with pe.Fori(3, SHARED - 2, 2) as u:
                g1(u, 1, 0, 0)
                g2(u - 1, 0, 0, 0)
                g1(u + 1, 0, 0, 0)
                g2(u, 1, 0, 0)
            g1(SHARED - 1, 1, 0, 0)
            transposes(0, 0, 16, first=True)
            g2(SHARED - 2, 0, 0, 0)
            slot(0, 0)
            slot(1, 1)
            with pe.Fori(2, SLOTS - 3, 2) as s:
                slot(s, 0, static=False)
                slot(s + 1, 1, static=False)
            slot(SLOTS - 2, 0)
            slot(SLOTS - 1, 1)
            g2(SHARED + SLOTS - 1, 1, 0, SLOTS)

        @block.vector
        def _(dve):
            done = [0]

            def step(ins):
                done[0] += 1
                ins.then_inc(s_ro, 1)
                dve.wait_ge(s_ro, done[0])

            def w1l(v, par):
                dve.wait_ge(s_w1h, v + 1)
                dve.tensor_tensor(w1_lo[:, par], raw1[:], w1_hi[:, par].bitcast(F32), ALU.subtract).then_inc(s_w1l, 1)

            def w2l(v, par):
                dve.wait_ge(s_w2h, v + 1)
                dve.tensor_tensor(w2_lo[:, par], raw2[:], w2_hi[:, par].bitcast(F32), ALU.subtract).then_inc(s_w2l, 1)

            def xl(u, par, shared):
                dve.wait_ge(s_xh, u + 1)
                src = xT[:, :, bass.ds(u * T, T)] if shared else XB.rearrange("p (c t) -> p c t", c=2)
                dve.tensor_tensor(x_lo[:, par], src, x_hi[:, par].bitcast(F32), ALU.subtract).then_inc(s_xl, 1)

            def h1l(u, par, pairs):
                for j in pairs:
                    dve.wait_ge(s_hhi, PAIRS1 * u + j + 1)
                    dve.tensor_tensor(h1_lo[:, par, 2 * j:2 * j + 2, :], h1[:, 2 * j:2 * j + 2, :],
                                      h1_hi[:, par, 2 * j:2 * j + 2, :].bitcast(F32), ALU.subtract).then_inc(s_hlo, 1)

            def h1h(u, par, pairs):
                dve.wait_ge(s_g2, u - 1)
                for j in pairs:
                    dve.wait_ge(s_silu, PAIRS1 * u + j + 1)
                    dve.tensor_copy(h1_hi[:, par, 2 * j:2 * j + 2, :], h1[:, 2 * j:2 * j + 2, :]).then_inc(s_hhi, 1)

            def y_shared(u, par):
                dve.wait_ge(s_g2, u + 1)
                dve.tensor_tensor(acc[:, bass.ds(2 * u, 2), :], G2[par].rearrange("p (j c) -> p j c", j=2),
                                  acc[:, bass.ds(2 * u, 2), :], ALU.add).then_inc(s_y, 1)

            def y_slot(s, par, first=False):
                dve.wait_ge(s_g2, SHARED + s + 1)
                if not first:
                    dve.wait_ge(s_store[par], 8 * s - 8 * par)
                e = dve.value_load(slot_e[0:1, bass.ds(s, 1)], min_val=0, max_val=E - 1)
                dve.tensor_tensor(y[:, par], G2[par].rearrange("p (j c) -> p j c", j=2),
                                  b2_rows[:, bass.ds(e, 1), :].broadcast_to([P, 2, M]), ALU.add).then_inc(s_y, 1)

            def slot(s, par, static=True):
                if static and s < 2:
                    y_shared(SHARED + s - 2, par)
                else:
                    y_slot(s - 2, par, first=static and s < 4)
                h1h(SHARED + s, par, (0, 1))
                last = static and s == SLOTS - 1
                if not last:
                    w1l(s + 2, par)
                h1h(SHARED + s, par, (2, 3))
                if not last:
                    xl(SHARED + s + 1, 1 - par, False)
                w2l(s + 1, 1 - par)

            def over(ap, n):
                return ap.unsqueeze(2).broadcast_to([P, TILES, n])

            def tiles_of(ap):
                return ap.unsqueeze(1).broadcast_to([P, TILES, E])

            w1l(0, 0)
            xl(0, 0, True)
            xl(1, 1, True)
            dve.wait_ge(s_logit, 1)
            step(dve.tensor_tensor(logit[:], RB[:, 0:128].rearrange("p (t e) -> p t e", e=E), tiles_of(br2[:]), ALU.add))
            step(dve.tensor_scalar(rev[:], RAMP[:, 0:E], -1.0, float(E), ALU.mult, ALU.add))
            step(dve.tensor_reduce(col[:], logit[:], X, ALU.max))
            step(dve.tensor_tensor(logit[:], logit[:], over(col[:], E), ALU.subtract))
            assert done[0] == SOFT
            dve.wait_ge(s_soft, 1)
            step(dve.tensor_reduce(col[:], logit[:], X, ALU.add))
            step(dve.reciprocal(col2[:], col[:]))
            step(dve.tensor_tensor(logit[:], logit[:], over(col2[:], E), ALU.mult))
            for k in range(2):
                step(dve.tensor_reduce(best[k][:], logit[:], X, ALU.max))
                step(dve.tensor_tensor(eq[:], logit[:], over(best[k][:], E), ALU.is_equal))
                step(dve.tensor_tensor(key[:], eq[:], tiles_of(rev[:]), ALU.mult))
                step(dve.tensor_reduce(col[:], key[:], X, ALU.max))
                step(dve.tensor_tensor(pick[k][:], key[:], over(col[:], E), ALU.is_equal))
                if k == 0:
                    step(dve.scalar_tensor_tensor(logit[:], pick[0][:], -2.0, logit[:], ALU.mult, ALU.add))
            step(dve.tensor_tensor(both[:], pick[0][:], pick[1][:], ALU.add))
            step(dve.tensor_reduce(n_exp[:], both[:].rearrange("p t e -> p e t"), X, ALU.add))
            dve.engine_nop().then_inc(s_picked, 1)
            step(dve.tensor_tensor(col2[:], best[1][:], best[0][:], ALU.subtract))
            assert done[0] == SOFT2
            dve.wait_ge(s_soft, 2)
            step(dve.tensor_scalar(col[:], col2[:], 1.0, None, ALU.add))
            step(dve.reciprocal(gate_w[:, 0, :], col[:]))
            step(dve.tensor_tensor(gate_w[:, 1, :], col2[:], gate_w[:, 0, :], ALU.mult))
            dve.wait_ge(s_rank, 1)
            step(dve.tensor_copy(n_exp[:], RB[:, 256:256 + E]))
            step(dve.tensor_scalar(end_e[:], RAMP[:, 0:E], float(T), None, ALU.mult))
            step(dve.tensor_tensor(cmp[:, 0:E, :], n_exp[:].unsqueeze(2).broadcast_to([P, E, E]),
                                   end_e[:].unsqueeze(1).broadcast_to([P, E, E]), ALU.is_gt))
            step(dve.tensor_reduce(slots_e[:], cmp[:, 0:E, :], X, ALU.add))
            step(dve.tensor_tensor(cmp[:, 0:E, :], UPTO, slots_e[:].unsqueeze(1).broadcast_to([P, E, E]), ALU.mult))
            step(dve.tensor_reduce(end_e[:], cmp[:, 0:E, :], X, ALU.add))
            step(dve.tensor_tensor(base_e[:], end_e[:], slots_e[:], ALU.subtract))
            step(dve.tensor_scalar(base_e[:], base_e[:], float(T), None, ALU.mult))
            step(dve.tensor_tensor(rank[:], RB[:, 128:256].rearrange("p (t e) -> p t e", e=E), tiles_of(base_e[:]), ALU.add))
            for k in range(2):
                step(dve.tensor_tensor(key[:], rank[:], pick[k][:], ALU.mult))
                step(dve.tensor_reduce(col[:], key[:], X, ALU.add))
                step(dve.tensor_copy(pos[:, k, :], col[:]))
            step(dve.tensor_tensor(cmp[:, 0:SLOTS, :], end_e[:].unsqueeze(1).broadcast_to([P, SLOTS, E]),
                                   RAMP[:, 0:SLOTS].unsqueeze(2).broadcast_to([P, SLOTS, E]), ALU.is_le))
            step(dve.tensor_reduce(slot_f[:], cmp[:, 0:SLOTS, :], X, ALU.add))
            step(dve.tensor_scalar(slot_f[:], slot_f[:], float(E - 1), None, ALU.min))
            dve.tensor_copy(slot_e[:], slot_f[:]).then_inc(s_pos, 1)

            dve.wait_ge(s_acc0, 4)
            h1l(0, 0, range(PAIRS1))
            w2l(0, 0)
            h1l(1, 1, range(PAIRS1))
            xl(2, 0, True)
            y_shared(0, 0)
            h1l(2, 0, range(PAIRS1))
            xl(3, 1, True)
            with dve.Fori(3, SHARED - 2, 2) as u:
                y_shared(u - 2, 1)
                h1l(u, 1, range(PAIRS1))
                xl(u + 1, 0, True)
                y_shared(u - 1, 0)
                h1l(u + 1, 0, range(PAIRS1))
                xl(u + 2, 1, True)
            y_shared(SHARED - 3, 1)
            h1l(SHARED - 1, 1, range(PAIRS1))
            w1l(1, 1)
            xl(SHARED, 0, False)
            for s in range(4):
                slot(s, s % 2)
            with dve.Fori(4, SLOTS - 3, 2) as s:
                slot(s, 0, static=False)
                slot(s + 1, 1, static=False)
            for s in range(SLOTS - 2, SLOTS):
                slot(s, s % 2)
            y_slot(SLOTS - 2, 0)
            y_slot(SLOTS - 1, 1)

            for q in range(4):
                for t in range(4 * q, 4 * q + 4):
                    for k in range(2):
                        n = 2 * t + k
                        dve.wait_ge(s_rows[n % GR], 16 * (n // GR + 1))
                        if k:
                            dve.wait_ge(s_mix, n)
                        dve.scalar_tensor_tensor(acc[:, t, :], rows[:, n % GR, :], gate_w[:, k, t:t + 1],
                                                 acc[:, t, :], ALU.mult, ALU.add).then_inc(s_mix, 1)
                for t in range(4 * q, 4 * q + 4):
                    dve.wait_ge(s_mix, 2 * t + 2)
                    dve.bn_stats(stats[:, t, :], acc[:, t, :]).then_inc(s_st, 1)
                for t in range(4 * q, 4 * q + 4):
                    dve.wait_ge(s_st, t + 1)
                    dve.bn_aggr(mv[:, t, :], stats[:, t, :]).then_inc(s_mv, 1)
                dve.wait_ge(s_sd, q + 1)
                dve.reciprocal(rstd[:, 4 * q:4 * q + 4], sd[:, 4 * q:4 * q + 4]).then_inc(s_rstd, 1)
                dve.wait_ge(s_rstd, q + 1)
                for t in range(4 * q, 4 * q + 4):
                    ts = dve.tensor_scalar(acc[:, t, :], acc[:, t, :], mv[:, t, 0:1], rstd[:, t:t + 1],
                                           ALU.subtract, ALU.mult)
                ts.then_inc(s_fin, 1)


def build(nc, A, out):
    with ExitStack() as ctx:
        def sb(name, shape, dt=F32):
            return ctx.enter_context(nc.sbuf_tensor(name, shape, dt))

        keep = {"hln": sb("hln", [P, TILES, M]), "xT": sb("xT", [P, 2, TOKENS]),
                "small": sb("small", [P, SMALL]), "eps": sb("eps", [P, 1]),
                "raw1": sb("raw1", [P, 2, I]), "raw2": sb("raw2", [P, IC, M]),
                "scratch": sb("scratch", [P, TOKENS]), "wr1": sb("wr1", [P, 2, R1]), "br1": sb("br1", [R1, 1]),
                "wr2": sb("wr2", [R1, E]), "br2": sb("br2", [P, E]), "b1_in": sb("b1_in", [(E + 1) * IC, P]),
                "b2_rows": sb("b2_rows", [P, E + 1, M])}
        keep["psum"] = ctx.enter_context(nc.psum_tensor("psum", [P, 8, 512], F32))[:]
        keep["bank"] = [keep["psum"][:, i, :] for i in range(8)]
        for n in ("s_raw1", "s_raw2", "s_zero", "s_early", "s_relu"):
            keep[n] = ctx.enter_context(nc.semaphore(n))
        front(nc, A, keep)
        experts(nc, A, keep, out)


def kernel(**inputs):
    import concourse.bacc as bacc
    from concourse.bass_utils import run_bass_kernel_spmd

    nc = bacc.Bacc("TRN2", target_bir_lowering=False, num_devices=1)
    given = {k.split("_", 2)[-1] if k.startswith("L0") else k: np.asarray(v) for k, v in inputs.items()}
    dft, small = shape_constants()
    tables = {"dft_table": dft, "small_table": small}
    for n in ("x", "scharr", "A_log", "D", "C_re", "log_dt", "Wr1", "br1", "Wr2", "br2"):
        tables[n] = given[n]
    for n in ("W1", "b1", "W2", "b2"):
        tables[n] = np.concatenate([given[n[0] + "e" + n[1]], given[n[0] + "s" + n[1]][None]])
    arrays, A = {}, {}
    for n, a in tables.items():
        arrays[f"in_{n}_dram"] = np.ascontiguousarray(a)
        A[n] = nc.dram_tensor(f"in_{n}_dram", a.shape, mybir.dt.from_np(a.dtype), kind="ExternalInput").ap()
    for n in ("xs_d", "ys_d"):
        A[n] = nc.dram_tensor(n, (SLOTS * T, M), F32, kind="Internal").ap()
    out = nc.dram_tensor("out_dram", (B, L, M), F32, kind="ExternalOutput").ap()
    build(nc, A, out)
    r = run_bass_kernel_spmd(nc, [arrays], core_ids=[0])
    return r.results[0]["out_dram"]
```

```python
from contextlib import ExitStack

import concourse.bass as bass
import numpy as np
from concourse import mybir

F32 = mybir.dt.float32
F32R = mybir.dt.float32r
I32 = mybir.dt.int32
U32 = mybir.dt.uint32
ALU = mybir.AluOpType
ACT = mybir.ActivationFunctionType
X = mybir.AxisListType.X

P = 128
B, COLORS, L, M = 8, 3, 256, 256
LH = L // P
TILES = B * LH
PAIRS = B // 2
W2 = 2 * M
N_STATE = 64
MP = M // 2
Q = 16
NB = L // Q
GRAY = (0.2989, 0.587, 0.114)
EPS = 1e-5

TOKENS = B * L
E, K_TOP = 8, 2
I, IC = 1024, 8
PAIRS1 = IC // 2
R1 = M // 4
T = 256
SHARED = TOKENS // T
FIRST = 5
SLOTS = K_TOP * TOKENS // T + E - 1
LAST = FIRST + SLOTS
UNITS = SHARED + SLOTS
assert SLOTS % 2 == 1 and FIRST % 2 == 1 and FIRST < SHARED
EARLY = 7 * P + 2
SMALL = EARLY + 2 * P + E * E + K_TOP * TILES + SLOTS * T // P
XM = M + 1
PARAMS = (("log_dt", MP), ("A_log", 1), ("taps", 18), ("seam_taps", 2), ("C_re", 2 * N_STATE))
XS_ROWS = (SLOTS + 1) * T
ZPARTS = 12
SOFT, GAP = 4, 21


def shape_constants():
    pos, freq = np.arange(P)[:, None], np.arange(P)[None, :]

    def waves(n, k):
        ang = np.pi * (n * (2 * k + 1) % (4 * P)) / (2 * P)
        return [np.cos(ang), -np.sin(ang)]

    behind = [w * (pos > 0) for w in waves(pos - P, freq)]
    inverse = [w / P for w in waves(freq, pos)]
    dft = np.stack(waves(pos, freq) + behind + inverse, 1)
    row, col = pos, freq
    bands = [(row - col == dy - 1) for dy in range(3)]
    ramp = np.broadcast_to(col, (P, P))
    seam = np.zeros((P, 2, P))
    seam[0:9, 0, P - 1] = 1
    seam[9:18, 1, 0] = 1
    is_lo = pos // 3 % 3 == 2
    upto = np.broadcast_to((np.arange(E)[None, :] <= np.arange(E)[:, None]).reshape(1, -1), (P, E * E))
    place = SLOTS * T + np.arange(K_TOP)[None, :, None] * TOKENS + np.arange(TILES) * P + pos[:, :, None]
    small = np.concatenate([np.stack(bands + [row == col, ramp], 1).reshape(P, -1), seam.reshape(P, -1),
                            1 - is_lo, is_lo, row < col, np.ones((P, P)), upto, place.reshape(P, -1),
                            np.arange(SLOTS * T // P) * P + pos], 1)
    return np.ascontiguousarray(dft.reshape(P, -1), np.float32), np.ascontiguousarray(small, np.float32)


def front(nc, A, keep):
    xT, scratch = keep["xT"], keep["scratch"]
    hln = keep["hrow"][:, :, 0:M]
    small, eps_t, bank, wr1, br1 = keep["small"], keep["eps"], keep["bank"], keep["wr1"], keep["br1"]
    BAND = [small[:, i * P:(i + 1) * P] for i in range(3)]
    IDENT = small[:, 3 * P:4 * P]
    RAMP = small[:, 4 * P:5 * P]
    SEAM = [small[0:18, (5 + i) * P:(6 + i) * P] for i in range(2)]
    IS_HI, IS_LO = small[0:18, EARLY - 2:EARLY - 1], small[0:18, EARLY - 1:EARLY]
    with ExitStack() as ctx:
        def sb(name, shape, dt=F32):
            return ctx.enter_context(nc.sbuf_tensor(name, shape, dt))

        def sem(name):
            return ctx.enter_context(nc.semaphore(name))

        NX = 3
        image = sb("image", [P, NX, COLORS, LH, M])
        gray = sb("gray", [P, 2, LH, 4, M + 2], F32R)
        edge_rows = sb("edge_rows", [18, 2, 2, M + 2], F32R)
        dft = sb("dft", [P, 6, P])
        params = sb("params", [P, sum(n for _, n in PARAMS)])
        param, at = {}, 0
        for name, n in PARAMS:
            param[name] = params[:, at:at + n]
            at += n
        taps = param["taps"].rearrange("p (f y x) -> p f y x", f=2, y=3)
        seam_taps = param["seam_taps"][0:18]
        stencil = sb("stencil", [P, 2, 2, 3, P], F32R)
        seam = sb("seam", [18, 2, 2, P], F32R)
        seam_split = sb("seam_split", [18, 3, 2])
        half_abs = sb("half_abs", [P, 2, 2, W2])
        h = sb("h", [P, LH, PAIRS, W2])
        log_dt, a_log = param["log_dt"], param["A_log"]
        a_exp = sb("a_exp", [P, 1])
        dt_exp = sb("dt_exp", [P, MP])
        neg_dta = sb("neg_dta", [P, MP])
        far = sb("far", [P, MP, NB])
        c_in = param["C_re"]
        d_row = sb("d_row", [1, M])
        zero = sb("zero", [P, XS_ROWS * XM // P // ZPARTS])
        taps_k = sb("taps_k", [P, LH, M])
        kf = sb("kf", [P, 2, 3, M])
        prod = sb("prod", [P, 3, 2, 2, W2])
        specs = [sb("spec", [P, 3, 2, W2]),
                 image[:].rearrange("p n c q m -> p (n c q m)")[:, 0:6 * W2].rearrange("p (k r w) -> p k r w", k=3, r=2)]
        stats = sb("stats", [P, TILES, 6])
        mv = sb("mv", [P, TILES, 2])
        sd = sb("sd", [P, TILES])
        rstd = sb("rstd", [P, TILES])
        shift = sb("shift0", [P, TILES])
        stencil_parts = prod[:].rearrange("p a b c w -> p (a b c w)")[:, 0:18 * P].rearrange(
            "p (y f x l) -> p y f x l", y=3, f=2, x=3)
        decay = scratch[:].rearrange("p (m q) -> p m q", q=Q)
        c_decay = keep["hrow"][:].rearrange("p t m -> p (t m)")[:, 0:2 * MP * NB].rearrange("p (m h b) -> p m h b", h=2, b=NB)
        kq = xT[0:Q].rearrange("q a (b m) -> q (a b) m", m=M)
        r1T = scratch[0:R1, :]

        s_image = [sem(f"s_image{i}") for i in range(NX)]
        s_const, s_param, s_late = sem("s_const"), sem("s_param"), sem("s_late")
        s_pad = sem("s_pad")
        s_gray1 = sem("s_gray1")
        s_gray2 = sem("s_gray2")
        s_gray = sem("s_gray")
        s_ghi, s_glo = sem("s_ghi"), sem("s_glo")
        s_sth, s_seam, s_seam_st = sem("s_sth"), sem("s_seam"), sem("s_seam_st")
        s_rows = [sem(f"s_rows{i}") for i in range(PAIRS)]
        s_st0, s_stencil = sem("s_st0"), sem("s_stencil")
        s_edge = sem("s_edge")
        s_abs, s_h = sem("s_abs"), sem("s_h")
        s_exp0, s_dta, s_farg, s_far = sem("s_exp0"), sem("s_dta"), sem("s_farg"), sem("s_far")
        s_ct, s_cz, s_cd = sem("s_ct"), sem("s_cz"), sem("s_cd")
        s_arg, s_decay, s_ksum = sem("s_arg"), sem("s_decay"), sem("s_ksum")
        s_kq, s_relay, s_kd, s_kf, s_kfc = sem("s_kq"), sem("s_relay"), sem("s_kd"), sem("s_kf"), sem("s_kfc")
        s_u = sem("s_u")
        s_prod, s_diff, s_spec = sem("s_prod"), sem("s_diff"), sem("s_spec")
        s_y = sem("s_y")
        s_stat, s_mv, s_sd, s_rstd = sem("s_stat"), sem("s_mv"), sem("s_sd"), sem("s_rstd")
        s_shift = sem("s_shift0")
        s_ln = sem("s_ln")
        s_xt, s_xtc = sem("s_xt"), sem("s_xtc")
        s_r1 = sem("s_r1")
        s_early = keep["s_early"]

        EDGE = [bank[0], bank[1]]
        YB = [bank[2], bank[3]]
        XT = [YB] + 3 * [EDGE]
        HID = [bank[4], bank[5], bank[6], bank[4]]
        LOGITS = keep["logits"]
        KFB = YB
        SPECTRA = keep["psum"][:, 4:8, :]
        KSUM = [bank[4 + i] for i in range(4)]
        KCH = 512 // (2 * NB)
        block = ctx.enter_context(nc.Block())

        @block.sync
        def _(sp):
            x = A["x"]

            def load_image(b):
                if b >= NX:
                    sp.wait_ge(s_glo, b - NX + 1)
                sp.dma_start(image[:, b % NX], x[b].rearrange("c (q p) m -> p (c q) m", p=P)
                             ).then_inc(s_image[b % NX], 16)

            def seam_rows(g):
                sp.wait_ge(s_pad, 2)
                sp.wait_ge(s_glo, 2 * g + 2)
                if g >= 2:
                    sp.wait_ge(s_edge, 4 * g - 4)
                n = 2 * (M + 2) - 2
                for k, (p, lh) in enumerate(((0, 1), (P - 1, 0))):
                    for e, part in enumerate((0, 1, 0)):
                        row = gray[p:p + 1, part, lh, 2 * (g % 2), :].bitcast(F32)
                        windows = bass.AP(row.tensor, row.offset, [list(row.ap[0]), [1, 3], [1, n]])
                        r = 9 * k + 3 * e
                        to = edge_rows[r:r + 3, g % 2].rearrange("r b m -> r (b m)")[:, 0:n].bitcast(F32)
                        sp.dma_start(to, windows).then_inc(s_rows[g], 16)

            sp.dma_start(small[:, 0:EARLY], A["small_table"][:, 0:EARLY]).then_inc(s_const, 16)
            for b in range(NX):
                load_image(b)
            load_image(3)
            load_image(4)
            seam_rows(0)
            sp.wait_ge(s_kq, MP // KCH)
            for i in range(P // Q):
                sp.dma_start(taps_k[Q * i:Q * i + Q, :, :], kq[:, i::P // Q, :]).then_inc(s_relay, 16)
            load_image(5)
            seam_rows(1)
            load_image(6)
            load_image(7)
            seam_rows(2)
            sp.dma_start(keep["raw1"][:], A["W1"][E].rearrange("(c p) i -> p c i", p=P)).then_inc(keep["s_raw1"], 16)
            sp.dma_start(keep["raw2"][:], A["W2"][E].rearrange("(a p) c -> p a c", p=P)).then_inc(keep["s_raw2"], 16)
            seam_rows(3)
            n = zero.shape[1]
            sp.wait_ge(s_pad, 4)
            for i in range(ZPARTS):
                sp.dma_start(A["xs_d"].rearrange("(p r) c -> p (r c)", p=P)[:, i * n:(i + 1) * n], zero[:]
                             ).then_inc(keep["s_zero"], 16)
            sp.wait_ge(keep["s_zero"], ZPARTS * 16)

        @block.gpsimd
        def _(pool):
            pads = gray[:].bitcast(F32).rearrange("p a h b m -> p (a h b) m")
            pool.memset(pads[:, :, 0:1], 0.0).then_inc(s_pad, 1)
            pool.memset(pads[:, :, M + 1:M + 2], 0.0).then_inc(s_pad, 1)
            pool.memset(c_decay, 0.0).then_inc(s_cz, 1)
            pool.memset(eps_t[:], EPS).then_inc(s_pad, 1)
            pool.wait_ge(s_const, 16)
            pool.wait_ge(s_dta, 1)
            pool.tensor_tensor(far[:], neg_dta[:].unsqueeze(2).broadcast_to([P, MP, NB]),
                               RAMP[:, 0:NB].unsqueeze(1).broadcast_to([P, MP, NB]), ALU.mult).then_inc(s_farg, 1)
            for c in range(2):
                part = slice(c * MP // 2, (c + 1) * MP // 2)
                pool.tensor_tensor(decay[:, part, :], neg_dta[:, part].unsqueeze(2).broadcast_to([P, MP // 2, Q]),
                                   RAMP[:, 0:Q].unsqueeze(1).broadcast_to([P, MP // 2, Q]), ALU.mult).then_inc(s_arg, 1)
            pool.memset(zero[:], 0.0).then_inc(s_pad, 1)

            def sum_filters(n):
                g, lh = n // 2, n % 2
                pool.wait_ge(s_abs, 2 * n + 2)
                pool.tensor_tensor(h[:, lh, g, :], half_abs[:, lh, 0, :], half_abs[:, lh, 1, :],
                                   ALU.add).then_inc(s_h, 1)

            def sum_products(g, ks):
                spec = specs[g % 2]
                for k in ks:
                    pool.wait_ge(s_prod, 6 * g + 2 * k + 2)
                    if g == 1 and k == 0:
                        pool.wait_ge(s_glo, B)
                    if g >= 2 and k == 0:
                        pool.wait_ge(s_y, LH * (g - 1))
                    pool.tensor_tensor(spec[:, k, 0, :], prod[:, k, 0, 0, :], prod[:, k, 0, 1, :],
                                       ALU.subtract).then_inc(s_diff, 1)
                    pool.tensor_tensor(spec[:, k, 1, :], prod[:, k, 1, 0, :], prod[:, k, 1, 1, :],
                                       ALU.add).then_inc(s_diff, 1)
                    if k == 2:
                        pool.wait_ge(s_diff, 6 * g + 6)
                        pool.tensor_tensor(spec[:, 2], spec[:, 1], spec[:, 2], ALU.add).then_inc(s_spec, 1)

            for n in range(3):
                sum_filters(n)
            sum_products(0, (0,))
            sum_filters(3)
            sum_products(0, (1, 2))
            sum_filters(4)
            sum_products(1, (0, 1))
            sum_filters(5)
            sum_products(1, (2,))
            sum_products(2, (0,))
            sum_filters(6)
            sum_products(2, (1, 2))
            sum_filters(7)
            sum_products(3, (0, 1, 2))

        @block.scalar
        def _(act):
            act.dma_start(params[:], A["params"]).then_inc(s_param, 16)
            act.dma_start(small[:, EARLY:], A["small_table"][:, EARLY:]).then_inc(s_late, 16)
            act.dma_start(d_row[:], A["D"].rearrange("(a m) -> a m", a=1)).then_inc(s_late, 16)
            act.dma_start(dft[:].rearrange("p a b -> p (a b)"), A["dft_table"]).then_inc(s_late, 16)

            def gray_first(b):
                act.wait_ge(s_image[b % NX], 16 * (b // NX + 1))
                act.activation(image[:, b % NX, 0], image[:, b % NX, 0], ACT.Copy, scale=GRAY[0]).then_inc(s_gray1, 1)

            def gray_hi(b):
                act.wait_ge(s_gray, b + 1)
                if b >= 4:
                    act.wait_ge(s_edge, 4 * (b // 2) - 4)
                act.activation(gray[:, 0, :, b % 4, 1:M + 1], image[:, b % NX, 0], ACT.Copy).then_inc(s_ghi, 1)

            def abs_edges(n):
                for f in range(2):
                    act.wait_ge(s_edge, 2 * n + f + 1)
                    if n >= 2:
                        act.wait_ge(s_h, n - 1)
                    act.activation(half_abs[:, n % 2, f, :], EDGE[f], ACT.Abs, scale=0.5).then_inc(s_abs, 1)

            def deviation(g):
                act.wait_ge(s_mv, 4 * g + 4)
                act.activation(sd[:, 4 * g:4 * g + 4], mv[:, 4 * g:4 * g + 4, 1], ACT.Sqrt,
                               bias=eps_t[:, 0:1]).then_inc(s_sd, 1)

            def normalise(g):
                act.wait_ge(s_shift, g + 1)
                for lh in range(LH):
                    for b in range(2):
                        t = 4 * g + 2 * b + lh
                        ins = act.activation(hln[:, t, :], YB[lh][:, b * M:(b + 1) * M], ACT.Identity,
                                             bias=shift[:, t:t + 1], scale=rstd[:, t:t + 1])
                ins.then_inc(s_ln, 1)

            def copy_xt(g):
                for c in range(2):
                    act.wait_ge(s_xt, 2 * g + c + 1)
                    act.activation(xT[:, c, g * W2:(g + 1) * W2], XT[g][c], ACT.Copy).then_inc(s_xtc, 1)

            def relu(g):
                act.wait_ge(s_r1, g + 1)
                act.activation(r1T[:, g * W2:(g + 1) * W2], HID[g][0:R1, :], ACT.Relu,
                               bias=br1[:, 0:1]).then_inc(keep["s_relu"], 1)

            act.wait_ge(s_param, 16)
            act.activation(a_exp[:], a_log, ACT.Exp).then_inc(s_exp0, 1)
            act.activation(dt_exp[:], log_dt, ACT.Exp).then_inc(s_exp0, 1)
            act.activation(seam_split[:, 0, :].bitcast(F32R), seam_taps, ACT.Copy).then_inc(s_seam, 1)
            gray_first(0)
            gray_first(1)
            act.wait_ge(s_st0, 5)
            act.activation(stencil[:, 0], stencil_parts[:, 0], ACT.Copy).then_inc(s_sth, 1)
            gray_hi(0)
            gray_hi(1)
            act.wait_ge(s_farg, 1)
            act.activation(far[:], far[:], ACT.Exp, scale=float(Q)).then_inc(s_far, 1)
            for c in range(2):
                act.wait_ge(s_arg, c + 1)
                part = decay[:, c * MP // 2:(c + 1) * MP // 2, :]
                act.activation(part, part, ACT.Exp).then_inc(s_decay, 1)
            gray_first(2)
            gray_first(3)
            for i in range(MP // KCH):
                act.wait_ge(s_ksum, i + 1)
                act.activation(kq.rearrange("q b (h m) -> q m h b", h=2)[:, i * KCH:(i + 1) * KCH],
                               KSUM[i % 4][0:Q, :].rearrange("q (m h b) -> q m h b", h=2, b=NB), ACT.Copy).then_inc(s_kq, 1)
            abs_edges(0)
            gray_hi(2)
            gray_hi(3)
            abs_edges(1)
            gray_first(4)
            abs_edges(2)
            gray_first(5)
            gray_hi(4)
            gray_hi(5)
            for k in range(2):
                act.wait_ge(s_kf, k + 1)
                act.activation(kf[:, k, 0:2, :].rearrange("p a m -> p (a m)"), KFB[k], ACT.Copy).then_inc(s_kfc, 1)
                act.activation(kf[:, k, 2, :], KFB[k][:, 0:M], ACT.Copy).then_inc(s_kfc, 1)
            abs_edges(3)
            act.dma_start(wr1[:], A["Wr1"].rearrange("(c p) r -> p c r", p=P)).then_inc(s_early, 16)
            act.dma_start(br1[:], A["br1"].rearrange("(r a) -> r a", a=1)).then_inc(s_early, 16)
            act.dma_start(keep["wr2"][:], A["Wr2"]).then_inc(s_early, 16)
            act.dma_start(keep["br2"][:], A["br2"].partition_broadcast(P)).then_inc(s_early, 16)
            act.dma_start(keep["b1_in"][:], A["b1"].rearrange("e (a p) -> (e a) p", p=P)).then_inc(s_early, 16)
            act.dma_start(keep["b2_rows"][:].rearrange("p e m -> p (e m)"),
                          A["b2"].rearrange("e m -> (e m)").partition_broadcast(P)).then_inc(s_early, 16)
            gray_first(6)
            gray_first(7)
            gray_hi(6)
            gray_hi(7)
            abs_edges(4)
            abs_edges(5)
            act.wait_ge(s_pad, 3)
            deviation(0)
            normalise(0)
            abs_edges(6)
            copy_xt(0)
            abs_edges(7)
            act.wait_ge(s_early, 96)
            deviation(1)
            normalise(1)
            copy_xt(1)
            deviation(2)
            normalise(2)
            relu(0)
            relu(1)
            copy_xt(2)
            relu(2)
            deviation(3)
            normalise(3)
            copy_xt(3)
            relu(3)

        @block.tensor
        def _(pe):
            def edges(n):
                edges_inside(n)
                edges_seam(n)

            def edges_inside(n):
                g, lh = n // 2, n % 2
                if lh == 0:
                    pe.wait_ge(s_glo, 2 * g + 2)
                b = 2 * (g % 2)
                for f in range(2):
                    if n:
                        pe.wait_ge(s_abs, 2 * n - 1 + f)
                    for st, x in ((0, 0), (0, 1), (1, 0)):
                        for dx in range(3):
                            pe.matmul(EDGE[f], stencil[:, st, f, dx, :], gray[:, x, lh, b:b + 2, dx:dx + M],
                                      start=(st + x + dx == 0), stop=False)

            def edges_seam(n):
                g, lh = n // 2, n % 2
                if n == 0:
                    pe.wait_ge(s_seam_st, 2 * LH)
                pe.wait_ge(s_rows[g], 16 * 6)
                for f in range(2):
                    pe.matmul(EDGE[f], seam[:, f, lh, :], edge_rows[:, g % 2, :, 0:M],
                              start=False, stop=True).then_inc(s_edge, 1)

            def spectra(g):
                for j in range(2):
                    pe.wait_ge(s_h, 2 * g + j + 1)
                    if g:
                        pe.wait_ge(s_prod, 6 * (g - 1) + (4 if j == 0 else 6))
                    for ri in range(2):
                        mm = pe.matmul(SPECTRA[:, 2 * j + ri, :], dft[:, ri, :], h[:, j, g, :], start=True, stop=True)
                    mm.then_inc(s_u, 1)

            def convolved(g):
                if g == 0:
                    pe.wait_ge(s_kfc, 4)
                elif g == 1:
                    pe.wait_ge(s_xtc, 2)
                else:
                    pe.wait_ge(s_ln, g)
                for lh in range(LH):
                    if lh == 0:
                        pe.wait_ge(s_diff, 6 * g + 2)
                    else:
                        pe.wait_ge(s_spec, g + 1)
                    for ri in range(2):
                        mm = pe.matmul(YB[lh], dft[:, 4 + ri, :], specs[g % 2][:, 2 * lh, ri, :], start=(ri == 0), stop=(ri == 1))
                    mm.then_inc(s_y, 1)

            def transposes(g):
                pe.wait_ge(s_ln, g + 1)
                if g == 1:
                    pe.wait_ge(s_abs, 4 * PAIRS)
                elif g > 1:
                    pe.wait_ge(s_xtc, 2 * g)
                for c in range(2):
                    for t in range(4):
                        mm = pe.transpose(XT[g][c][:, t * P:(t + 1) * P], hln[:, 4 * g + t, c * P:(c + 1) * P], IDENT)
                    mm.then_inc(s_xt, 1)

            def hidden(g):
                if g == 0:
                    pe.wait_ge(s_early, 96)
                    pe.wait_ge(s_prod, 6 * PAIRS)
                elif g == 3:
                    pe.wait_ge(keep["s_relu"], 1)
                pe.wait_ge(s_xtc, 2 * g + 2)
                for c in range(2):
                    mm = pe.matmul(HID[g][0:R1, :], wr1[:, c, :], xT[:, c, g * W2:(g + 1) * W2],
                                   start=(c == 0), stop=(c == 1))
                mm.then_inc(s_r1, 1)

            def logits(g):
                pe.wait_ge(keep["s_relu"], g + 1)
                for t in range(4 * g, 4 * g + 4):
                    mm = pe.matmul(LOGITS[:, t * E:(t + 1) * E], r1T[:, t * P:(t + 1) * P], keep["wr2"][:],
                                   start=True, stop=True)
                mm.then_inc(keep["s_logit"], 1)

            pe.wait_ge(s_const, 16)
            pe.wait_ge(s_param, 16)
            pe.transpose(bank[2][:, 0:P], c_in, IDENT).then_inc(s_ct, 1)
            pe.wait_ge(s_stencil, 1)
            pe.wait_ge(s_pad, 2)
            edges_inside(0)
            pe.wait_ge(s_cd, 2)
            for mp in range(MP):
                if mp % (MP // 2) == 0:
                    pe.wait_ge(s_decay, mp // (MP // 2) + 1)
                i, n = mp // KCH, mp % KCH
                if n == 0 and i >= 4:
                    pe.wait_ge(s_kq, i - 3)
                mm = pe.matmul(KSUM[i % 4][0:Q, 2 * NB * n:2 * NB * (n + 1)], decay[:, mp, :],
                               c_decay[:, mp].rearrange("p h b -> p (h b)"), start=True, stop=True)
                if n == KCH - 1:
                    mm.then_inc(s_ksum, 1)
            edges_seam(0)
            edges(1)
            edges(2)
            pe.wait_ge(s_kd, 1)
            pe.wait_ge(s_late, 48)
            for ri in range(2):
                mm = pe.matmul(KFB[0][:, ri * M:(ri + 1) * M], dft[:, ri, :], taps_k[:, 0, :], start=True, stop=True)
            mm.then_inc(s_kf, 1)
            for ri in range(2):
                pe.matmul(KFB[1][:, ri * M:(ri + 1) * M], dft[:, 2 + ri, :], taps_k[:, 0, :], start=True, stop=False)
                mm = pe.matmul(KFB[1][:, ri * M:(ri + 1) * M], dft[:, ri, :], taps_k[:, 1, :], start=False, stop=True)
            mm.then_inc(s_kf, 1)
            spectra(0)
            edges(3)
            edges(4)
            spectra(1)
            edges(5)
            convolved(0)
            spectra(2)
            edges(6)
            transposes(0)
            edges(7)
            convolved(1)
            spectra(3)
            transposes(1)
            convolved(2)
            hidden(0)
            hidden(1)
            transposes(2)
            logits(0)
            convolved(3)
            hidden(2)
            logits(1)
            logits(2)
            transposes(3)
            hidden(3)
            logits(3)

        @block.vector
        def _(dve):
            dve.wait_ge(s_param, 16)
            dve.wait_ge(s_const, 16)
            for dy in range(3):
                dve.tensor_tensor(stencil_parts[:, dy], BAND[dy].unsqueeze(1).unsqueeze(1).broadcast_to([P, 2, 3, P]),
                                  taps[:, :, dy, :].unsqueeze(3).broadcast_to([P, 2, 3, P]), ALU.mult).then_inc(s_st0, 1)
            dve.wait_ge(s_exp0, 2)
            dve.tensor_scalar(neg_dta[:], dt_exp[:], a_exp[:, 0:1], -1.0, ALU.mult, ALU.mult).then_inc(s_dta, 1)
            for dy in (1, 2):
                dve.wait_ge(s_st0, 2 + dy)
                dve.tensor_tensor(stencil_parts[:, 0], stencil_parts[:, 0], stencil_parts[:, dy], ALU.add).then_inc(s_st0, 1)
            def gray_rest(b):
                dve.wait_ge(s_gray1, b + 1)
                gray0 = image[:, b % NX, 0]
                for c in (1, 2):
                    if c == 2:
                        dve.wait_ge(s_gray2, b + 1)
                    dve.scalar_tensor_tensor(gray0, image[:, b % NX, c], GRAY[c], gray0, ALU.mult, ALU.add
                                             ).then_inc(s_gray2 if c == 1 else s_gray, 1)

            def gray_lo(b):
                dve.wait_ge(s_ghi, b + 1)
                dve.tensor_tensor(gray[:, 1, :, b % 4, 1:M + 1], image[:, b % NX, 0],
                                  gray[:, 0, :, b % 4, 1:M + 1].bitcast(F32), ALU.subtract).then_inc(s_glo, 1)

            gray_rest(0)
            gray_rest(1)
            dve.wait_ge(s_sth, 1)
            dve.tensor_tensor(stencil[:, 1], stencil_parts[:, 0], stencil[:, 0].bitcast(F32), ALU.subtract
                              ).then_inc(s_stencil, 1)
            gray_lo(0)
            gray_lo(1)
            dve.wait_ge(s_seam, 1)
            dve.tensor_tensor(seam_split[:, 1, :], seam_taps, seam_split[:, 0, :], ALU.subtract).then_inc(s_seam, 1)
            dve.wait_ge(s_seam, 2)
            dve.tensor_scalar(seam_split[:, 2, :], seam_split[:, 0, :], IS_HI, None, ALU.mult).then_inc(s_seam, 1)
            dve.wait_ge(s_seam, 3)
            dve.scalar_tensor_tensor(seam_split[:, 2, :], seam_split[:, 1, :], IS_LO, seam_split[:, 2, :],
                                     ALU.mult, ALU.add).then_inc(s_seam, 1)
            dve.wait_ge(s_seam, 4)
            for f in range(2):
                for lh in range(LH):
                    dve.tensor_scalar(seam[:, f, lh, :], SEAM[lh], seam_split[:, 2, f:f + 1], None,
                                      ALU.mult).then_inc(s_seam_st, 1)
            dve.wait_ge(s_ct, 1)
            dve.wait_ge(s_cz, 1)
            dve.wait_ge(s_far, 1)
            for mh in range(2):
                r = slice(64 * mh, 64 * mh + 64)
                dve.tensor_tensor(c_decay[r, :, mh, :], bank[2][r, 0:P].unsqueeze(2).broadcast_to([64, MP, NB]),
                                  far[r], ALU.mult).then_inc(s_cd, 1)
            gray_rest(2)
            gray_rest(3)
            gray_lo(2)
            gray_lo(3)
            gray_rest(4)
            dve.wait_ge(s_relay, 16 * P // Q)
            dve.wait_ge(s_late, 48)
            dve.scalar_tensor_tensor(taps_k[0:1, 0], d_row[:], 1.0, taps_k[0:1, 0], ALU.add, ALU.add
                                     ).then_inc(s_kd, 1)

            def products(g):
                for n, (k, j) in enumerate(((0, 0), (1, 0), (0, 1))):
                    dve.wait_ge(s_u, 2 * g + j + 1)
                    if g:
                        dve.wait_ge(s_diff, 6 * (g - 1) + 2 * n + 2)
                    for kind in range(2):
                        dve.tensor_tensor(prod[:, n, kind].rearrange("p r (b m) -> p r b m", b=2),
                                          SPECTRA[:, 2 * j:2 * j + 2, :].rearrange("p r (b m) -> p r b m", b=2),
                                          kf[:, k, kind:kind + 2, :].unsqueeze(2).broadcast_to([P, 2, 2, M]),
                                          ALU.mult).then_inc(s_prod, 1)

            def moments(g):
                for lh in range(LH):
                    dve.wait_ge(s_y, LH * g + lh + 1)
                    for b in range(2):
                        t = 4 * g + 2 * b + lh
                        dve.bn_stats(stats[:, t, :], YB[lh][:, b * M:(b + 1) * M]).then_inc(s_stat, 1)
                dve.wait_ge(s_stat, 4 * g + 4)
                for t in range(4 * g, 4 * g + 4):
                    dve.bn_aggr(mv[:, t, :], stats[:, t, :]).then_inc(s_mv, 1)

            def scale(g):
                ts = slice(4 * g, 4 * g + 4)
                dve.wait_ge(s_sd, g + 1)
                dve.reciprocal(rstd[:, ts], sd[:, ts]).then_inc(s_rstd, 1)
                dve.wait_ge(s_rstd, g + 1)
                dve.scalar_tensor_tensor(shift[:, ts], mv[:, ts, 0], -1.0, rstd[:, ts], ALU.mult, ALU.mult
                                         ).then_inc(s_shift, 1)

            gray_rest(5)
            gray_lo(4)
            gray_lo(5)
            dve.wait_ge(s_kfc, 4)
            products(0)
            gray_rest(6)
            gray_rest(7)
            gray_lo(6)
            gray_lo(7)
            products(1)
            moments(0)
            scale(0)
            products(2)
            moments(1)
            scale(1)
            products(3)
            moments(2)
            scale(2)
            moments(3)
            scale(3)


def experts(nc, A, keep, out):
    hrow, xT, small, eps_t, bank = (keep[k] for k in ("hrow", "xT", "small", "eps", "bank"))
    hln = hrow[:, :, 0:M]
    raw1, raw2, s_raw1, s_raw2 = (keep[k] for k in ("raw1", "raw2", "s_raw1", "s_raw2"))
    br2, b1_in, b2_rows = (keep[k] for k in ("br2", "b1_in", "b2_rows"))
    RAMP, BEFORE, ONES = small[:, 4 * P:5 * P], small[:, EARLY:EARLY + P], small[:, EARLY + P:EARLY + 2 * P]
    IDENT = small[:, 3 * P:4 * P]
    END = EARLY + 2 * P + E * E
    UPTO = small[:, END - E * E:END].rearrange("p (e f) -> p e f", f=E)
    PLACE = small[:, END:END + K_TOP * TILES].rearrange("p (k t) -> p k t", k=K_TOP)
    EMPTY = small[:, END + K_TOP * TILES:].rearrange("p (s j) -> p s j", s=SLOTS)
    with ExitStack() as ctx:
        def sb(name, shape, dt=F32):
            return ctx.enter_context(nc.sbuf_tensor(name, shape, dt))

        def sem(name):
            return ctx.enter_context(nc.semaphore(name))

        b1T = sb("b1T", [P, (E + 1) * IC])
        b1_now = sb("b1_now", [P, 2, IC])
        w1_hi, w1_lo = sb("w1_hi", [P, 2, 2, I], F32R), sb("w1_lo", [P, 2, 2, I], F32R)
        w2_hi, w2_lo = sb("w2_hi", [P, 2, IC, M], F32R), sb("w2_lo", [P, 2, IC, M], F32R)
        x_hi, x_lo = sb("x_hi", [P, 2, 2, T], F32R), sb("x_lo", [P, 2, 2, T], F32R)
        h1 = keep["scratch"][:].rearrange("p (a t) -> p a t", t=T)
        h1_hi, h1_lo = sb("h1_hi", [P, 2, IC, T], F32R), sb("h1_lo", [P, 2, IC, T], F32R)
        xs, y = sb("xs", [P, 2, 2, XM]), sb("y", [P, 2, 2, M])
        places = sb("places", [P, SLOTS, 2])
        place_now = sb("place_now", [P, 2, 2], I32)
        raw1_rows = raw1[:].rearrange("p c (r m) -> p c r m", m=M)
        rows = [raw1_rows[:, 0], raw1_rows[:, 1], raw2[:, 0:4, :], raw2[:, 4:8, :],
                y[:].rearrange("p a j m -> p (a j) m")]
        acc = sb("acc", [P, TILES, M])

        def rt(name, shape=(P, TILES, E), dt=F32):
            return sb(name, list(shape), dt)
        logit, eq, key, rank = rt("logit"), rt("eq"), rt("key"), rt("rank")
        pick = [rt("pick0"), rt("pick1")]
        best = [rt("best0", (P, TILES)), rt("best1", (P, TILES))]
        both = rt("both")
        col, col2 = rt("col", (P, TILES)), rt("col2", (P, TILES))
        gate_w = rt("gate_w", (P, 2, TILES))
        rev = rt("rev", (P, E))
        n_exp, slots_e, end_e, base_e = (rt(n, (P, E)) for n in ("n_exp", "slots_e", "end_e", "base_e"))
        cmp = rt("cmp", (P, max(SLOTS, E), E))
        pos = rt("pos", (P, 2, TILES), I32)
        slot_f = rt("slot_f", (P, SLOTS))
        slot_e = rt("slot_e", (P, SLOTS), I32)
        stats, mv = sb("stats2", [P, TILES, 6]), sb("mv2", [P, TILES, 2])
        sd, rstd, shift = (sb(n, [P, TILES]) for n in ("sd2", "rstd2", "shift"))

        s_b1t, s_b1c = sem("s_b1t"), sem("s_b1c")
        s_soft = sem("s_soft")
        s_ro = sem("s_ro")
        s_picked = sem("s_picked")
        s_rank = sem("s_rank")
        s_pos = sem("s_pos")
        s_acc0 = sem("s_acc0")
        s_scat = [sem("s_scat0"), sem("s_scat1")]
        s_w1h, s_w1l, s_w2h, s_w2l = sem("s_w1h"), sem("s_w1l"), sem("s_w2h"), sem("s_w2l")
        s_xs = [sem("s_xs0"), sem("s_xs1")]
        s_xt, s_xh, s_xl = sem("s_xt2"), sem("s_xh"), sem("s_xl")
        s_bias = sem("s_bias")
        s_part_h, s_part_l = sem("s_part_h"), sem("s_part_l")
        s_g1, s_silu, s_hhi, s_hlo, s_g2 = sem("s_g1"), sem("s_silu"), sem("s_hhi"), sem("s_hlo"), sem("s_g2")
        s_y = sem("s_y2")
        s_sent = [sem("s_sent0"), sem("s_sent1")]
        s_place = sem("s_place")
        s_own = sem("s_own")
        s_rows = [sem(f"s_rows2_{i}") for i in range(len(rows))]
        s_mix = sem("s_mix")
        s_weighed = sem("s_weighed")
        s_mix2 = sem("s_mix2")
        s_st, s_mv, s_sd, s_rstd, s_fin = sem("s_st2"), sem("s_mv2"), sem("s_sd2"), sem("s_rstd2"), sem("s_fin")
        s_shift, s_fin_last = sem("s_shift"), sem("s_fin_last")
        s_out = sem("s_out")

        G2 = [bank[4], bank[5]]
        XB, RB = bank[6], bank[7]
        xs_d, ys_d = A["xs_d"], A["ys_d"]
        BATCHES = ((0, 8), (8, 16))
        STORES = ((0, 8), (8, 12), (12, 16))
        block = ctx.enter_context(nc.Block())

        LOADS = ((0, 0), (6, 1), (1, 2), (7, 3), (2, 4), (3, 0), (4, 1), (5, 2))
        POOL_IMAGES, DVE_IMAGES = (6, 7, 4), (0, 1, 2, 3, 5)
        BUFFER = dict(LOADS)

        def loaded(b):
            n = [i for i, _ in LOADS].index(b)
            return 16 * K_TOP * [buffer for _, buffer in LOADS[:n + 1]].count(BUFFER[b])

        @block.sync
        def _(sp):
            def load_w1(v, e):
                sp.wait_ge(s_w1l, v)
                sp.dma_start(raw1[:], A["W1"][e].rearrange("(c p) i -> p c i", p=P)).then_inc(s_raw1, 16)

            def load_w2(v, e):
                sp.wait_ge(s_w2l, v)
                sp.dma_start(raw2[:], A["W2"][e].rearrange("(a p) c -> p a c", p=P)).then_inc(s_raw2, 16)

            def load_x(s, par, first=False):
                if not first:
                    sp.wait_ge(s_place, s - 1)
                sp.dma_start(xs[:, par], xs_d[bass.ds(s * T, T), :].rearrange("(j p) c -> p j c", p=P)
                             ).then_inc(s_xs[par], 16)

            def expert_of(s):
                return sp.value_load(slot_e[0:1, bass.ds(s, 1)], min_val=0, max_val=E - 1)

            def slot(s, par, static=True):
                if static and s + 1 == SLOTS:
                    load_w1(s + 2, E)
                else:
                    load_w1(s + 2, expert_of(s + 1))
                    load_x(s + 1, 1 - par, first=static and s == 0)
                load_w2(s + 1, expert_of(s))

            sp.wait_ge(s_pos, 1)
            load_w1(1, expert_of(0))
            for i in range(2):
                sp.wait_ge(s_scat[i], 16 * K_TOP * TILES // 2)
            load_x(0, 0, first=True)
            slot(0, 0)
            slot(1, 1)
            with sp.Fori(2, SLOTS - 2, 2) as s:
                slot(s, 0, static=False)
                slot(s + 1, 1, static=False)
            slot(SLOTS - 1, 0)
            load_w2(SLOTS + 1, E)
            sp.wait_ge(s_w1l, SLOTS + 2)
            sp.wait_ge(s_w2l, SLOTS + 2)
            for par in range(2):
                sp.wait_ge(s_sent[par], 32 * ((SLOTS + 1 - par) // 2))
            for n, (b, buffer) in enumerate(LOADS):
                for before in [i for i, other in LOADS[:n] if other == buffer]:
                    if before in POOL_IMAGES:
                        sp.wait_ge(s_mix2, 2 * (POOL_IMAGES.index(before) + 1))
                    else:
                        sp.wait_ge(s_mix, 4 * (DVE_IMAGES.index(before) + 1))
                for k in range(K_TOP):
                    r0 = SLOTS * T + k * TOKENS + b * L
                    sp.dma_start(rows[buffer][:, 2 * k:2 * k + 2, :],
                                 ys_d[r0:r0 + L, :].rearrange("(j p) c -> p j c", p=P)).then_inc(s_rows[buffer], 16)
            for n, (t0, t1) in enumerate(STORES):
                if n + 1 < len(STORES):
                    sp.wait_ge(s_fin, n + 1)
                else:
                    sp.wait_ge(s_fin_last, 1)
                sp.dma_start(out[t0 // 2:t1 // 2].rearrange("b (h p) m -> p (b h) m", p=P), acc[:, t0:t1, :]
                             ).then_inc(s_out, 16)
            sp.wait_ge(s_out, 16 * len(STORES))

        @block.gpsimd
        def _(pool):
            for t in range(0, TILES, 4):
                pool.tensor_tensor(acc[:, t:t + 4, :], hln[:, t:t + 4, :],
                                   b2_rows[:, E:E + 1, :].broadcast_to([P, 4, M]), ALU.add).then_inc(s_acc0, 1)
            pool.tensor_copy(hrow[:, :, M], PLACE[:, 0, :]).then_inc(s_own, 1)
            pool.wait_ge(s_own, 1)
            pool.wait_ge(s_pos, 1)
            for k in range(K_TOP):
                for i in range(2):
                    ts = range(i * TILES // 2, (i + 1) * TILES // 2)
                    if k:
                        pool.wait_ge(s_scat[i], 16 * len(ts))
                        pool.tensor_copy(hrow[:, ts[0]:ts[-1] + 1, M], PLACE[:, 1, ts[0]:ts[-1] + 1]).then_inc(s_own, 1)
                        pool.wait_ge(s_own, i + 2)
                    for t in ts:
                        pool.indirect_dma_start(xs_d, bass.IndirectOffsetOnAxis(ap=pos[:, k, t:t + 1].bitcast(U32), axis=0),
                                                hrow[:, t, :], None).then_inc(s_scat[i], 16)

            def lo(u, par, pairs):
                for j in pairs:
                    pool.wait_ge(s_hhi, PAIRS1 * u + j + 1)
                    pool.tensor_tensor(h1_lo[:, par, 2 * j:2 * j + 2, :], h1[:, 2 * j:2 * j + 2, :],
                                       h1_hi[:, par, 2 * j:2 * j + 2, :].bitcast(F32), ALU.subtract).then_inc(s_hlo, 1)

            def send(s, par):
                for j in range(2):
                    pool.indirect_dma_start(ys_d, bass.IndirectOffsetOnAxis(ap=place_now[:, par, j:j + 1].bitcast(U32), axis=0),
                                            y[:, par, j, :], None).then_inc(s_sent[par], 16)

            lo(FIRST, 1, range(PAIRS1))
            lo(FIRST + 1, 0, range(PAIRS1))

            def slot(s, par):
                lo(FIRST + s, 1 - par, (0,))
                pool.wait_ge(s_y, FIRST + s - 1)
                lo(FIRST + s, 1 - par, (1,))
                send(s - 2, par)
                lo(FIRST + s, 1 - par, (2, 3))

            with pool.Fori(2, SLOTS - 2, 2) as s:
                slot(s, 0)
                slot(s + 1, 1)
            slot(SLOTS - 1, 0)
            pool.wait_ge(s_y, LAST - 1)
            send(SLOTS - 2, 1)
            pool.wait_ge(s_y, LAST)
            send(SLOTS - 1, 0)
            for n, b in enumerate(POOL_IMAGES):
                pool.wait_ge(s_rows[BUFFER[b]], loaded(b))
                now, both_tiles = rows[BUFFER[b]], slice(2 * b, 2 * b + 2)
                for k in range(K_TOP):
                    part = now[:, 2 * k:2 * k + 2, :]
                    pool.tensor_tensor(part, part, gate_w[:, k, both_tiles].unsqueeze(2).broadcast_to([P, 2, M]),
                                       ALU.mult).then_inc(s_weighed, 1)
                for k in range(K_TOP):
                    pool.wait_ge(s_weighed, 2 * n + k + 1)
                    if k:
                        pool.wait_ge(s_mix2, 2 * n + 1)
                    pool.tensor_tensor(acc[:, both_tiles, :], acc[:, both_tiles, :], now[:, 2 * k:2 * k + 2, :],
                                       ALU.add).then_inc(s_mix2, 1)

        @block.scalar
        def _(act):
            def w1h(v, par, first=False):
                act.wait_ge(s_raw1, 16 * v + 16)
                if not first:
                    act.wait_ge(s_g1, PAIRS1 * (v + FIRST - 2))
                act.activation(w1_hi[:, par], raw1[:], ACT.Copy).then_inc(s_w1h, 1)

            def w2h(v, par, first=False):
                act.wait_ge(s_raw2, 16 * v + 16)
                if not first:
                    act.wait_ge(s_g2, v + FIRST - 2)
                act.activation(w2_hi[:, par], raw2[:], ACT.Copy).then_inc(s_w2h, 1)

            def xh(u, par, group=None, first=False):
                if not first:
                    act.wait_ge(s_g1, PAIRS1 * (u - 1))
                if group is None:
                    act.wait_ge(s_xt, u - FIRST + 1)
                    src = XB.rearrange("p (c t) -> p c t", c=2)
                else:
                    src = xT[:, :, group * T:(group + 1) * T]
                act.activation(x_hi[:, par], src, ACT.Copy).then_inc(s_xh, 1)

            def silu(u, par, pairs, bias, shared, first=False):
                for j in pairs:
                    act.wait_ge(s_g1, PAIRS1 * u + j + 1)
                    if not first:
                        act.wait_ge(s_hlo, PAIRS1 * (u - 1) + j + 1)
                    for a in range(2):
                        ic = 2 * j + a
                        ins = act.activation(h1[:, ic, :], bank[j][:, a * T:(a + 1) * T], ACT.Silu,
                                             bias=bias[:, ic:ic + 1])
                    ins.then_inc(s_silu, 1)
                    if shared:
                        act.wait_ge(s_silu, PAIRS1 * u + j + 1)
                        act.activation(h1_hi[:, par, 2 * j:2 * j + 2, :], h1[:, 2 * j:2 * j + 2, :], ACT.Copy
                                       ).then_inc(s_hhi, 1)

            def shared_unit(u, par, first=False):
                b = b1T[:, E * IC:(E + 1) * IC]
                if not first:
                    act.wait_ge(s_g2, u - 1)
                silu(u, par, range(PAIRS1), b, True, first)

            def slot(s, par, last=False):
                u = FIRST + s
                e = act.value_load(slot_e[0:1, bass.ds(s, 1)], min_val=0, max_val=E - 1)
                act.activation(b1_now[:, par, :], b1T[:, bass.ds(e * IC, IC)], ACT.Copy).then_inc(s_bias, 1)
                act.wait_ge(s_bias, s + 1)
                silu(u, 1 - par, (0, 1), b1_now[:, par, :], False)
                w1h(s + 2, par)
                silu(u, 1 - par, (2, 3), b1_now[:, par, :], False)
                xh(u + 1, par, FIRST if last else None)
                w2h(s + 1, 1 - par)

            xh(0, 0, 0, first=True)
            act.wait_ge(s_raw1, 16)
            for j in range(PAIRS1):
                i = slice(2 * P * j, 2 * P * (j + 1))
                act.activation(w1_hi[:, 0, :, i], raw1[:, :, i], ACT.Copy).then_inc(
                    s_part_h if j + 1 < PAIRS1 else s_w1h, 1)
            act.wait_ge(s_ro, SOFT)
            act.activation(logit[:], logit[:], ACT.Exp).then_inc(s_soft, 1)
            xh(1, 1, 1, first=True)
            act.wait_ge(s_b1t, 1)
            act.activation(b1T[:], XB[:, 0:(E + 1) * IC], ACT.Copy).then_inc(s_b1c, 1)
            w2h(0, 0, first=True)
            act.wait_ge(s_b1c, 1)
            shared_unit(0, 0, first=True)
            act.wait_ge(s_ro, GAP)
            act.activation(col2[:], col2[:], ACT.Tanh, scale=0.25).then_inc(s_soft, 1)
            for u in range(1, FIRST):
                if u + 1 < FIRST:
                    xh(u + 1, (u + 1) % 2, u + 1)
                if u == 2:
                    act.wait_ge(s_pos, 1)
                    w1h(1, 1, first=True)
                shared_unit(u, u % 2)
            xh(FIRST, 1)
            slot(0, 0)
            slot(1, 1)
            with act.Fori(2, SLOTS - 2, 2) as s:
                slot(s, 0)
                slot(s + 1, 1)
            slot(SLOTS - 1, 0, last=True)
            act.wait_ge(s_hlo, PAIRS1 * LAST)
            for u in range(LAST, UNITS):
                shared_unit(u, u % 2)
                if u == LAST:
                    w2h(SLOTS + 1, 0)
                if u + 1 < UNITS:
                    xh(u + 1, (u + 1) % 2, u + 1 - SLOTS)

            def deviation(n):
                t0, t1 = BATCHES[n]
                act.wait_ge(s_mv, t1)
                act.activation(sd[:, t0:t1], mv[:, t0:t1, 1], ACT.Sqrt, bias=eps_t[:, 0:1]).then_inc(s_sd, 1)

            def normalise(n):
                t0, t1 = STORES[n]
                act.wait_ge(s_shift, n + 1)
                for t in range(t0, t1):
                    ins = act.activation(acc[:, t, :], acc[:, t, :], ACT.Identity, bias=shift[:, t:t + 1],
                                         scale=rstd[:, t:t + 1])
                ins.then_inc(s_fin, 1)

            deviation(0)
            normalise(0)
            deviation(1)
            normalise(1)

        @block.tensor
        def _(pe):
            def g1(u, par, wpar, version, first=False):
                if not first:
                    pe.wait_ge(s_w1l, version + 1)
                pe.wait_ge(s_xl, u + 1)
                for j in range(PAIRS1):
                    if first and j + 1 < PAIRS1:
                        pe.wait_ge(s_part_l, j + 1)
                    elif first:
                        pe.wait_ge(s_w1l, 1)
                    if not first:
                        pe.wait_ge(s_silu, PAIRS1 * (u - 1) + j + 1)
                    for a in range(2):
                        i0 = (2 * j + a) * P
                        parts = [(w, x) for w, x in ((w1_hi, x_hi), (w1_hi, x_lo), (w1_lo, x_hi))]
                        for n, (w, x) in enumerate(parts):
                            for c in range(2):
                                mm = pe.matmul(bank[j][:, a * T:(a + 1) * T], w[:, wpar, c, i0:i0 + P],
                                               x[:, par, c, :], start=(n == 0 and c == 0), stop=(n == 2 and c == 1))
                    mm.then_inc(s_g1, 1)

            def g2(u, par, wpar, version, first=False, tiles=(0, 1)):
                pe.wait_ge(s_w2l, version + 1)
                if not first:
                    pe.wait_ge(s_y, u - 1)
                pe.wait_ge(s_hlo, PAIRS1 * u + PAIRS1)
                for j in tiles:
                    for ic in range(IC):
                        for n, (h, w) in enumerate(((h1_hi, w2_hi), (h1_hi, w2_lo), (h1_lo, w2_hi))):
                            mm = pe.matmul(G2[par][:, j * M:(j + 1) * M], h[:, par, ic, j * P:(j + 1) * P],
                                           w[:, wpar, ic, :], start=(ic == 0 and n == 0), stop=(ic == IC - 1 and n == 2))
                if 1 in tiles:
                    mm.then_inc(s_g2, 1)

            def transposes(s, par, count, first=False):
                pe.wait_ge(s_xs[par], count)
                if not first:
                    pe.wait_ge(s_xl, FIRST + s)
                for c in range(2):
                    for j in range(2):
                        mm = pe.transpose(XB[:, c * T + j * P:c * T + (j + 1) * P],
                                          xs[:, par, j, c * P:(c + 1) * P], IDENT)
                mm.then_inc(s_xt, 1)

            def slot(s, par, static=True):
                g1(FIRST + s, 1 - par, 1 - par, s + 1)
                if not static or s + 1 < SLOTS:
                    transposes(s + 1, 1 - par, 8 * s + (16 if par == 0 else 24))
                g2(FIRST + s - 1, par, par, s, tiles=(1,) if static and s == 0 else (0, 1))

            pe.transpose(XB[:, 0:(E + 1) * IC], b1_in[:], IDENT[0:(E + 1) * IC, 0:(E + 1) * IC]).then_inc(s_b1t, 1)
            g1(0, 0, 0, 0, first=True)
            pe.wait_ge(s_picked, 1)
            pe.matmul(RB[:, 128:256], BEFORE, both[:].rearrange("p t e -> p (t e)"), start=True, stop=False)
            for t in range(TILES - 1):
                n = TILES - 1 - t
                pe.matmul(RB[:, 128 + (t + 1) * E:256], ONES, both[:, t:t + 1, :].broadcast_to([P, n, E]),
                          start=False, stop=(t == TILES - 2))
            pe.matmul(RB[:, 256:256 + E], ONES, n_exp[:], start=True, stop=True).then_inc(s_rank, 1)
            for u in range(1, FIRST):
                g1(u, u % 2, 0, 0)
                g2(u - 1, (u - 1) % 2, 0, 0, first=u <= 2)
            transposes(0, 0, 16, first=True)
            g2(FIRST - 1, 0, 0, 0, tiles=(0,))
            slot(0, 0)
            slot(1, 1)
            with pe.Fori(2, SLOTS - 2, 2) as s:
                slot(s, 0, static=False)
                slot(s + 1, 1, static=False)
            slot(SLOTS - 1, 0)
            g1(LAST, 0, 0, SLOTS + 1)
            g2(LAST - 1, 1, 1, SLOTS)
            for u in range(LAST + 1, UNITS):
                g1(u, u % 2, 0, SLOTS + 1)
                g2(u - 1, (u - 1) % 2, 0, SLOTS + 1)
            g2(UNITS - 1, (UNITS - 1) % 2, 0, SLOTS + 1)

        @block.vector
        def _(dve):
            done = [0]

            def step(ins):
                done[0] += 1
                ins.then_inc(s_ro, 1)
                dve.wait_ge(s_ro, done[0])

            def w1l(v, par):
                dve.wait_ge(s_w1h, v + 1)
                dve.tensor_tensor(w1_lo[:, par], raw1[:], w1_hi[:, par].bitcast(F32), ALU.subtract).then_inc(s_w1l, 1)

            def w2l(v, par):
                dve.wait_ge(s_w2h, v + 1)
                dve.tensor_tensor(w2_lo[:, par], raw2[:], w2_hi[:, par].bitcast(F32), ALU.subtract).then_inc(s_w2l, 1)

            def xl(u, par, group=None):
                dve.wait_ge(s_xh, u + 1)
                src = XB.rearrange("p (c t) -> p c t", c=2) if group is None else xT[:, :, group * T:(group + 1) * T]
                dve.tensor_tensor(x_lo[:, par], src, x_hi[:, par].bitcast(F32), ALU.subtract).then_inc(s_xl, 1)

            def h1l(u, par, pairs):
                for j in pairs:
                    dve.wait_ge(s_hhi, PAIRS1 * u + j + 1)
                    dve.tensor_tensor(h1_lo[:, par, 2 * j:2 * j + 2, :], h1[:, 2 * j:2 * j + 2, :],
                                      h1_hi[:, par, 2 * j:2 * j + 2, :].bitcast(F32), ALU.subtract).then_inc(s_hlo, 1)

            def h1h(u, par, pairs):
                dve.wait_ge(s_g2, u - 1)
                for j in pairs:
                    dve.wait_ge(s_silu, PAIRS1 * u + j + 1)
                    dve.tensor_copy(h1_hi[:, par, 2 * j:2 * j + 2, :], h1[:, 2 * j:2 * j + 2, :]).then_inc(s_hhi, 1)

            def y_shared(u, group):
                dve.wait_ge(s_g2, u + 1)
                dve.tensor_tensor(acc[:, 2 * group:2 * group + 2, :], G2[u % 2].rearrange("p (j c) -> p j c", j=2),
                                  acc[:, 2 * group:2 * group + 2, :], ALU.add).then_inc(s_y, 1)

            def y_slot(s, par, first=False):
                dve.wait_ge(s_g2, FIRST + s + 1)
                if not first:
                    dve.wait_ge(s_sent[par], 16 * s - 16 * par)
                dve.tensor_copy(place_now[:, par, :], places[:, bass.ds(s, 1), :])
                e = dve.value_load(slot_e[0:1, bass.ds(s, 1)], min_val=0, max_val=E - 1)
                dve.tensor_tensor(y[:, par], G2[1 - par].rearrange("p (j c) -> p j c", j=2),
                                  b2_rows[:, bass.ds(e, 1), :].broadcast_to([P, 2, M]), ALU.add).then_inc(s_y, 1)

            def place(s, par):
                dve.tensor_tensor(places[:, bass.ds(s, 1), :], xs[:, par, :, M].unsqueeze(1),
                                  EMPTY[:, bass.ds(s, 1), :], ALU.max).then_inc(s_place, 1)

            def slot(s, par, static=True):
                if static and s < 2:
                    y_shared(FIRST + s - 2, FIRST + s - 2)
                else:
                    y_slot(s - 2, par, first=static and s < 4)
                h1h(FIRST + s, 1 - par, (0, 1))
                w1l(s + 2, par)
                h1h(FIRST + s, 1 - par, (2, 3))
                xl(FIRST + s + 1, par, FIRST if static and s == SLOTS - 1 else None)
                if not static or s + 1 < SLOTS:
                    place(s + 1, 1 - par)
                w2l(s + 1, 1 - par)

            def over(ap, n):
                return ap.unsqueeze(2).broadcast_to([P, TILES, n])

            def tiles_of(ap):
                return ap.unsqueeze(1).broadcast_to([P, TILES, E])

            xl(0, 0, 0)
            dve.wait_ge(keep["s_logit"], PAIRS)
            step(dve.tensor_tensor(logit[:], keep["logits"].rearrange("p (t e) -> p t e", e=E), tiles_of(br2[:]), ALU.add))
            step(dve.tensor_scalar(rev[:], RAMP[:, 0:E], -1.0, float(E), ALU.mult, ALU.add))
            step(dve.tensor_reduce(col[:], logit[:], X, ALU.max))
            step(dve.tensor_tensor(logit[:], logit[:], over(col[:], E), ALU.subtract))
            assert done[0] == SOFT
            for j in range(PAIRS1):
                i = slice(2 * P * j, 2 * P * (j + 1))
                if j + 1 < PAIRS1:
                    dve.wait_ge(s_part_h, j + 1)
                else:
                    dve.wait_ge(s_w1h, 1)
                dve.tensor_tensor(w1_lo[:, 0, :, i], raw1[:, :, i], w1_hi[:, 0, :, i].bitcast(F32), ALU.subtract
                                  ).then_inc(s_part_l if j + 1 < PAIRS1 else s_w1l, 1)
            xl(1, 1, 1)
            dve.wait_ge(s_soft, 1)
            step(dve.tensor_reduce(col[:], logit[:], X, ALU.add))
            step(dve.reciprocal(col2[:], col[:]))
            step(dve.tensor_tensor(logit[:], logit[:], over(col2[:], E), ALU.mult))
            for k in range(2):
                step(dve.tensor_reduce(best[k][:], logit[:], X, ALU.max))
                step(dve.tensor_tensor(eq[:], logit[:], over(best[k][:], E), ALU.is_equal))
                step(dve.tensor_tensor(key[:], eq[:], tiles_of(rev[:]), ALU.mult))
                step(dve.tensor_reduce(col[:], key[:], X, ALU.max))
                step(dve.tensor_tensor(pick[k][:], key[:], over(col[:], E), ALU.is_equal))
                if k == 0:
                    step(dve.scalar_tensor_tensor(logit[:], pick[0][:], -2.0, logit[:], ALU.mult, ALU.add))
            step(dve.tensor_tensor(both[:], pick[0][:], pick[1][:], ALU.add))
            step(dve.tensor_reduce(n_exp[:], both[:].rearrange("p t e -> p e t"), X, ALU.add))
            dve.engine_nop().then_inc(s_picked, 1)
            step(dve.tensor_tensor(col2[:], best[0][:], best[1][:], ALU.subtract))
            assert done[0] == GAP
            h1l(0, 0, range(PAIRS1))
            w2l(0, 0)
            dve.wait_ge(s_rank, 1)
            step(dve.tensor_copy(n_exp[:], RB[:, 256:256 + E]))
            step(dve.tensor_scalar(end_e[:], RAMP[:, 0:E], float(T), None, ALU.mult))
            step(dve.tensor_tensor(cmp[:, 0:E, :], n_exp[:].unsqueeze(2).broadcast_to([P, E, E]),
                                   end_e[:].unsqueeze(1).broadcast_to([P, E, E]), ALU.is_gt))
            step(dve.tensor_reduce(slots_e[:], cmp[:, 0:E, :], X, ALU.add))
            step(dve.tensor_tensor(cmp[:, 0:E, :], UPTO, slots_e[:].unsqueeze(1).broadcast_to([P, E, E]), ALU.mult))
            step(dve.tensor_reduce(end_e[:], cmp[:, 0:E, :], X, ALU.add))
            step(dve.tensor_tensor(base_e[:], end_e[:], slots_e[:], ALU.subtract))
            step(dve.tensor_scalar(base_e[:], base_e[:], float(T), None, ALU.mult))
            step(dve.tensor_tensor(rank[:], RB[:, 128:256].rearrange("p (t e) -> p t e", e=E), tiles_of(base_e[:]), ALU.add))
            for k in range(2):
                step(dve.tensor_tensor(key[:], rank[:], pick[k][:], ALU.mult))
                step(dve.tensor_reduce(col[:], key[:], X, ALU.add))
                step(dve.tensor_copy(pos[:, k, :], col[:]))
            step(dve.tensor_tensor(cmp[:, 0:SLOTS, :], end_e[:].unsqueeze(1).broadcast_to([P, SLOTS, E]),
                                   RAMP[:, 0:SLOTS].unsqueeze(2).broadcast_to([P, SLOTS, E]), ALU.is_le))
            step(dve.tensor_reduce(slot_f[:], cmp[:, 0:SLOTS, :], X, ALU.add))
            step(dve.tensor_scalar(slot_f[:], slot_f[:], float(E - 1), None, ALU.min))
            dve.tensor_copy(slot_e[:], slot_f[:]).then_inc(s_pos, 1)

            dve.wait_ge(s_soft, 2)
            for k in range(2):
                step(dve.tensor_scalar(gate_w[:, k, :], col2[:], 0.5 - k, 0.5, ALU.mult, ALU.add))
            dve.wait_ge(s_acc0, 4)
            for u in range(1, FIRST):
                h1l(u, u % 2, range(PAIRS1))
                if u + 1 < FIRST:
                    xl(u + 1, (u + 1) % 2, u + 1)
                if u == 2:
                    w1l(1, 1)
                if u >= 1 and u < FIRST - 1:
                    y_shared(u - 1, u - 1)
            xl(FIRST, 1)
            place(0, 0)
            for s in range(4):
                slot(s, s % 2)
            with dve.Fori(4, SLOTS - 2, 2) as s:
                slot(s, 0, static=False)
                slot(s + 1, 1, static=False)
            slot(SLOTS - 1, 0)

            measured = []

            def moments(*tiles):
                for t in tiles:
                    dve.bn_stats(stats[:, t, :], acc[:, t, :]).then_inc(s_st, 1)
                for t in tiles:
                    measured.append(t)
                    dve.wait_ge(s_st, len(measured))
                    dve.bn_aggr(mv[:, t, :], stats[:, t, :]).then_inc(s_mv, 1)

            def mix(b):
                dve.wait_ge(s_rows[BUFFER[b]], loaded(b))
                for k in range(K_TOP):
                    if k:
                        dve.wait_ge(s_mix, 4 * DVE_IMAGES.index(b) + 2)
                    for j in range(2):
                        t = 2 * b + j
                        dve.scalar_tensor_tensor(acc[:, t, :], rows[BUFFER[b]][:, 2 * k + j, :],
                                                 gate_w[:, k, t:t + 1], acc[:, t, :], ALU.mult, ALU.add
                                                 ).then_inc(s_mix, 1)

            def scale(n):
                t0, t1 = BATCHES[n]
                dve.wait_ge(s_sd, n + 1)
                dve.reciprocal(rstd[:, t0:t1], sd[:, t0:t1]).then_inc(s_rstd, 1)
                dve.wait_ge(s_rstd, n + 1)
                dve.scalar_tensor_tensor(shift[:, t0:t1], mv[:, t0:t1, 0], -1.0, rstd[:, t0:t1], ALU.mult, ALU.mult
                                         ).then_inc(s_shift, 1)

            y_slot(SLOTS - 2, 1)
            h1l(LAST, LAST % 2, range(PAIRS1))
            w2l(SLOTS + 1, 0)
            xl(LAST + 1, 1, FIRST + 1)
            y_slot(SLOTS - 1, 0)
            h1l(LAST + 1, 1, range(PAIRS1))
            xl(LAST + 2, 0, FIRST + 2)
            dve.wait_ge(s_y, LAST)
            mix(0)
            y_shared(LAST, FIRST)
            dve.wait_ge(s_y, LAST + 1)
            mix(1)
            mix(2)
            h1l(LAST + 2, 0, range(0, 2))
            mix(3)
            h1l(LAST + 2, 0, range(2, PAIRS1))
            dve.wait_ge(s_mix, 4 * 4)
            moments(*range(8))
            mix(5)
            dve.wait_ge(s_mix2, 4)
            y_shared(LAST + 1, FIRST + 1)
            scale(0)
            dve.wait_ge(s_mix2, 6)
            dve.wait_ge(s_mix, 20)
            dve.wait_ge(s_y, LAST + 2)
            moments(*range(8, 14))
            y_shared(LAST + 2, FIRST + 2)
            dve.wait_ge(s_y, LAST + 3)
            moments(14, 15)
            scale(1)
            t0, t1 = STORES[2]
            dve.wait_ge(s_shift, 2)
            for t in range(t0, t1):
                ts = dve.tensor_scalar(acc[:, t, :], acc[:, t, :], rstd[:, t:t + 1], shift[:, t:t + 1], ALU.mult, ALU.add)
            ts.then_inc(s_fin_last, 1)


def build(nc, A, out):
    with ExitStack() as ctx:
        def sb(name, shape, dt=F32):
            return ctx.enter_context(nc.sbuf_tensor(name, shape, dt))

        keep = {"hrow": sb("hrow", [P, TILES, XM]), "xT": sb("xT", [P, 2, TOKENS]),
                "small": sb("small", [P, SMALL]), "eps": sb("eps", [P, 1]),
                "raw1": sb("raw1", [P, 2, I]), "raw2": sb("raw2", [P, IC, M]),
                "scratch": sb("scratch", [P, TOKENS]), "wr1": sb("wr1", [P, 2, R1]), "br1": sb("br1", [R1, 1]),
                "wr2": sb("wr2", [R1, E]), "br2": sb("br2", [P, E]), "b1_in": sb("b1_in", [(E + 1) * IC, P]),
                "b2_rows": sb("b2_rows", [P, E + 1, M])}
        keep["psum"] = ctx.enter_context(nc.psum_tensor("psum", [P, 8, 512], F32))[:]
        keep["logits"] = keep["psum"][:, 7, 0:TILES * E]
        keep["bank"] = [keep["psum"][:, i, :] for i in range(8)]
        for n in ("s_raw1", "s_raw2", "s_zero", "s_early", "s_relu", "s_logit"):
            keep[n] = ctx.enter_context(nc.semaphore(n))
        front(nc, A, keep)
        experts(nc, A, keep, out)


def pack_params(given):
    taps = given["scharr"][:, 0]
    seam = np.concatenate([np.tile(taps[:, dy].T, (3, 1)) for dy in (2, 0)])
    parts = {
        "log_dt": np.repeat(given["log_dt"].reshape(2, MP), N_STATE, 0),
        "A_log": np.tile(given["A_log"], 2)[:, None],
        "taps": np.broadcast_to(taps.reshape(1, -1), (P, 18)),
        "seam_taps": np.resize(seam, (P, 2)),
        "C_re": given["C_re"].reshape(2, MP, N_STATE).transpose(1, 0, 2).reshape(P, -1),
    }
    return np.concatenate([parts[n] for n, _ in PARAMS], 1)


def kernel(**inputs):
    import concourse.bacc as bacc
    from concourse.bass_utils import run_bass_kernel_spmd

    nc = bacc.Bacc("TRN2", target_bir_lowering=False, num_devices=1)
    given = {k.split("_", 2)[-1] if k.startswith("L0") else k: np.asarray(v) for k, v in inputs.items()}
    dft, small = shape_constants()
    tables = {"dft_table": dft, "small_table": small}
    for n in ("x", "D", "Wr1", "br1", "Wr2", "br2"):
        tables[n] = given[n]
    tables["params"] = pack_params(given)
    for n in ("W1", "b1", "W2", "b2"):
        tables[n] = np.concatenate([given[n[0] + "e" + n[1]], given[n[0] + "s" + n[1]][None]])
    arrays, A = {}, {}
    for n, a in tables.items():
        arrays[f"in_{n}_dram"] = np.ascontiguousarray(a)
        A[n] = nc.dram_tensor(f"in_{n}_dram", a.shape, mybir.dt.from_np(a.dtype), kind="ExternalInput").ap()
    for n, rows, cols in (("xs_d", XS_ROWS, XM), ("ys_d", SLOTS * T + K_TOP * TOKENS, M)):
        A[n] = nc.dram_tensor(n, (rows, cols), F32, kind="Internal").ap()
    out = nc.dram_tensor("out_dram", (B, L, M), F32, kind="ExternalOutput").ap()
    build(nc, A, out)
    r = run_bass_kernel_spmd(nc, [arrays], core_ids=[0])
    return r.results[0]["out_dram"]
```
